# Optimizing a Trainium2 kernel written in Bass

```python
import numpy as np
import jax
import jax.numpy as jnp

def _softmax(x, axis=-1):
    return jax.nn.softmax(x, axis=axis)

def _gelu(x):
    return jax.nn.gelu(x, approximate=True)

def _silu(x):
    return jax.nn.silu(x)

def _sigmoid(x):
    return jax.nn.sigmoid(x)

def _layernorm(x, axis=-1, eps=1e-05):
    m = jnp.mean(x, axis=axis, keepdims=True)
    v = jnp.var(x, axis=axis, keepdims=True)
    return (x - m) / jnp.sqrt(v + eps)

def _scatter_add(tgt, idx, src, axis=0):
    return tgt.at[idx].add(src)

def _segment_sum(src, seg, n):
    return jax.ops.segment_sum(src, seg, n)
kernel_name = 'mk_sandwich_d1_jaxref_r4_53243c'

def setup_inputs(seed: int=0):
    np.random.seed(seed)
    _w = jnp.asarray

    def _L0_attn_setup():
        import jax, jax.numpy as jnp
        import numpy as np
        EMBED_DIM = 512
        NUM_HEADS = 32
        HEAD_DIM = EMBED_DIM // NUM_HEADS
        BATCH = 2
        SEQ_LEN = 512
        key = jax.random.key(seed)
        ks = jax.random.split(key, 5)
        scale = 1.0 / np.sqrt(EMBED_DIM)
        x = jax.random.normal(ks[0], (BATCH, SEQ_LEN, EMBED_DIM), dtype=jnp.float32)
        Wq = jax.random.normal(ks[1], (EMBED_DIM, EMBED_DIM), dtype=jnp.float32) * scale
        Wk = jax.random.normal(ks[2], (EMBED_DIM, EMBED_DIM), dtype=jnp.float32) * scale
        Wv = jax.random.normal(ks[3], (EMBED_DIM, EMBED_DIM), dtype=jnp.float32) * scale
        Wo = jax.random.normal(ks[4], (EMBED_DIM, EMBED_DIM), dtype=jnp.float32) * scale
        return {'x': x, 'Wq': Wq, 'Wk': Wk, 'Wv': Wv, 'Wo': Wo}
    _L0_attn_in = _L0_attn_setup()

    def _L0_ffn_setup():
        import jax, jax.numpy as jnp
        import numpy as np
        HIDDEN = 512
        INTER = 2048
        COMPRESSION = 128.9

        def _n_ctrl(out_size, in_size):
            return max(16, int(out_size * in_size / COMPRESSION))

        def _catmull_rom_grid(n_ctrl, n_samples):
            t = np.linspace(0.0, n_ctrl - 1.0, n_samples, dtype=np.float64)
            i = np.clip(np.floor(t).astype(np.int64), 0, n_ctrl - 2)
            f = (t - i).astype(np.float32)
            idx = np.stack([np.clip(i + k, 0, n_ctrl - 1) for k in (-1, 0, 1, 2)], axis=0)
            return (jnp.asarray(idx.astype(np.int32)), jnp.asarray(f))

        def spline_reconstruct(control_points, out_size, in_size):
            n = out_size * in_size
            idx, f = _catmull_rom_grid(control_points.shape[0], n)
            p0, p1, p2, p3 = (control_points[idx[0]], control_points[idx[1]], control_points[idx[2]], control_points[idx[3]])
            f2 = f * f
            f3 = f2 * f
            w = 0.5 * (2.0 * p1 + (p2 - p0) * f + (2.0 * p0 - 5.0 * p1 + 4.0 * p2 - p3) * f2 + (3.0 * p1 - p0 - 3.0 * p2 + p3) * f3)
            return w.reshape(out_size, in_size)
        key = jax.random.key(seed)
        k0, k1, k2, k3 = jax.random.split(key, 4)
        hidden_states = jax.random.normal(k0, (4, 512, HIDDEN), dtype=jnp.float32)
        gate_cp = jax.random.normal(k1, (_n_ctrl(INTER, HIDDEN),), dtype=jnp.float32) * 0.02
        up_cp = jax.random.normal(k2, (_n_ctrl(INTER, HIDDEN),), dtype=jnp.float32) * 0.02
        down_cp = jax.random.normal(k3, (_n_ctrl(HIDDEN, INTER),), dtype=jnp.float32) * 0.02
        return {'hidden_states': hidden_states, 'gate_cp': gate_cp, 'up_cp': up_cp, 'down_cp': down_cp}
    _L0_ffn_in = _L0_ffn_setup()
    _d = {'L0_attn_x': _L0_attn_in['x'], 'L0_attn_Wq': _L0_attn_in['Wq'], 'L0_attn_Wk': _L0_attn_in['Wk'], 'L0_attn_Wv': _L0_attn_in['Wv'], 'L0_attn_Wo': _L0_attn_in['Wo'], 'L0_ffn_gate_cp': _L0_ffn_in['gate_cp'], 'L0_ffn_up_cp': _L0_ffn_in['up_cp'], 'L0_ffn_down_cp': _L0_ffn_in['down_cp']}
    _x0 = _d['L0_attn_x']
    _d['L0_attn_x'] = jax.random.normal(jax.random.fold_in(jax.random.key(seed), 1), (4, 1024, 512), dtype=_x0.dtype)
    del _x0
    return _d

def reference(L0_attn_x, L0_attn_Wq, L0_attn_Wk, L0_attn_Wv, L0_attn_Wo, L0_ffn_gate_cp, L0_ffn_up_cp, L0_ffn_down_cp):

    def _L0_attn_ref(x, Wq, Wk, Wv, Wo):
        import jax, jax.numpy as jnp
        import numpy as np
        EMBED_DIM = 512
        NUM_HEADS = 32
        HEAD_DIM = EMBED_DIM // NUM_HEADS
        BATCH = 2
        SEQ_LEN = 512
        q = jnp.einsum('bse,ef->bsf', x, Wq)
        k = jnp.einsum('bse,ef->bsf', x, Wk)
        v = jnp.einsum('bse,ef->bsf', x, Wv)
        qT = jnp.swapaxes(q, 1, 2)
        kT = jnp.swapaxes(k, 1, 2)
        vT = jnp.swapaxes(v, 1, 2)
        attn_scores = jnp.einsum('bes,bfs->bef', qT, kT) / np.sqrt(HEAD_DIM)
        attn_weights = jax.nn.softmax(attn_scores, axis=-1)
        attn_output = jnp.einsum('bef,bfs->bes', attn_weights, vT)
        attn_output = jnp.swapaxes(attn_output, 1, 2)
        return jnp.einsum('bse,ef->bsf', attn_output, Wo)

    def _L0_ffn_ref(hidden_states, gate_cp, up_cp, down_cp):
        import jax, jax.numpy as jnp
        import numpy as np
        HIDDEN = 512
        INTER = 2048
        COMPRESSION = 128.9

        def _n_ctrl(out_size, in_size):
            return max(16, int(out_size * in_size / COMPRESSION))

        def _catmull_rom_grid(n_ctrl, n_samples):
            t = np.linspace(0.0, n_ctrl - 1.0, n_samples, dtype=np.float64)
            i = np.clip(np.floor(t).astype(np.int64), 0, n_ctrl - 2)
            f = (t - i).astype(np.float32)
            idx = np.stack([np.clip(i + k, 0, n_ctrl - 1) for k in (-1, 0, 1, 2)], axis=0)
            return (jnp.asarray(idx.astype(np.int32)), jnp.asarray(f))

        def spline_reconstruct(control_points, out_size, in_size):
            n = out_size * in_size
            idx, f = _catmull_rom_grid(control_points.shape[0], n)
            p0, p1, p2, p3 = (control_points[idx[0]], control_points[idx[1]], control_points[idx[2]], control_points[idx[3]])
            f2 = f * f
            f3 = f2 * f
            w = 0.5 * (2.0 * p1 + (p2 - p0) * f + (2.0 * p0 - 5.0 * p1 + 4.0 * p2 - p3) * f2 + (3.0 * p1 - p0 - 3.0 * p2 + p3) * f3)
            return w.reshape(out_size, in_size)
        gate_w = spline_reconstruct(gate_cp, INTER, HIDDEN)
        up_w = spline_reconstruct(up_cp, INTER, HIDDEN)
        down_w = spline_reconstruct(down_cp, HIDDEN, INTER)
        gate = jnp.einsum('bsh,ih->bsi', hidden_states, gate_w)
        up = jnp.einsum('bsh,ih->bsi', hidden_states, up_w)
        inter = jax.nn.silu(gate) * up
        return jnp.einsum('bsi,hi->bsh', inter, down_w)
    x = L0_attn_x
    x = x + _layernorm(_L0_attn_ref(_layernorm(x, axis=-1), L0_attn_Wq, L0_attn_Wk, L0_attn_Wv, L0_attn_Wo), axis=-1)
    x = x + _layernorm(_L0_ffn_ref(_layernorm(x, axis=-1), L0_ffn_gate_cp, L0_ffn_up_cp, L0_ffn_down_cp), axis=-1)
    return x

_drawn_inputs = setup_inputs


def setup_inputs(seed=0):
    import zlib

    import numpy as np

    out = dict(_drawn_inputs(seed))
    spreads = {}
    factors = {}
    for name, (base, spread) in spreads.items():
        noise = np.random.default_rng([zlib.crc32(name.encode()), seed]).standard_normal(out[name].shape)
        drawn = base * np.exp(spread * noise) if base else spread * noise
        out[name] = jnp.asarray(drawn.astype(out[name].dtype))
    for name, factor in factors.items():
        out[name] = (out[name] * factor).astype(out[name].dtype)
    return out
```

```python
from contextlib import ExitStack

import concourse.bass as bass
from concourse import mybir

ALU = mybir.AluOpType
ACT = mybir.ActivationFunctionType
AX = mybir.AxisListType
F32 = mybir.dt.float32
F32R = mybir.dt.float32r
F16 = mybir.dt.float16

P = 128
EPS = 1e-5
XN_SCALE = 2.0 ** 11
BANK = 512


def f32(ap):
    return ap.bitcast(F32)


def held(engine, value):
    return value if isinstance(value, int) else engine.snap(value)


def attention_block(nc, x, wq, wk, wvT, wo, x1):
    B, S, E = x.shape
    K = E // P
    NT = S // P
    XR = 4
    CHAIN, EVACS, TB = 5 * K, 4 * K, K - 1 + K
    SELF = 2 * NT
    x_t = x.rearrange("b (t p) e -> (b t) p e", p=P)
    x1_t = x1.rearrange("(n p) e -> n p e", p=P)

    with ExitStack() as ctx:
        def sb(name, shape, dt):
            return ctx.enter_context(nc.sbuf_tensor(name, shape, dt))

        def psum(name, shape, dt):
            return ctx.enter_context(nc.psum_tensor(name, shape, dt))

        def sem(name):
            return ctx.enter_context(nc.semaphore(name))

        WK, WQ, WO, WV = range(4)
        w_stage = sb("w_stage", [P, 2, K, E], F32)
        w_hi = sb("w_hi", [P, 4, K, E], F32R)
        w_lo = sb("w_lo", [P, 4, K, E], F32R)
        x_in = sb("x_in", [P, XR, E], F32)
        xn = sb("xn", [P, 2, E], F32)
        xn_hi = sb("xn_hi", [P, NT, E], F16)
        xn_lo = sb("xn_lo", [P, NT, E], F16)
        xT_hi = sb("xT_hi", [P, K, S], F32R)
        xT_lo = sb("xT_lo", [P, K, S], F32R)
        ga_hi = sb("ga_hi", [P, K, E], F32R)
        ga_lo = sb("ga_lo", [P, K, E], F32R)
        tu_hi = sb("tu_hi", [P, K, E], F32R)
        tu_lo = sb("tu_lo", [P, K, E], F32R)
        m_hi = sb("m_hi", [P, K, E], F32R)
        m_lo = sb("m_lo", [P, K, E], F32R)
        expd = sb("expd", [P, 2, E], F32)
        x_res = sb("x_res", [P, XR, E], F32)
        y_n = sb("y_n", [P, 2, E], F32)
        ident32 = sb("ident32", [P, P], F32)
        ident16 = sb("ident16", [P, P], F16)
        stats = sb("stats", [P, 2, 6], F32)
        mv = sb("mv", [P, NT, 2], F32)
        rstd = sb("rstd", [P, NT, 2], F32)
        ystats = sb("ystats", [P, 2, 6], F32)
        ymv = sb("ymv", [P, NT, 2], F32)
        yr = sb("yr", [P, NT, 3], F32)
        smax = sb("smax", [P, K], F32)
        ssum = sb("ssum", [P, K], F32)
        srec = sb("srec", [P, K], F32)
        mhalf = sb("mhalf", [P, 1], F32)
        eps = sb("eps", [P, 1], F32)
        carrier = sb("carrier", [P, 1], F32)

        chain = psum("chain", [P, K, BANK], F32)
        ybank = psum("ybank", [P, 2, BANK], F32)
        tbank = psum("tbank", [P, 2, BANK], F32)

        s_ident = sem("s_ident")
        w_loaded = [sem(f"w_loaded{i}") for i in range(2)]
        w_hi_done = sem("w_hi_done")
        w_lo_done = sem("w_lo_done")
        x_loaded = [sem(f"x_loaded{i}") for i in range(XR)]
        res_loaded = [sem(f"res_loaded{i}") for i in range(XR)]
        x1_stored = [sem(f"x1_stored{i}") for i in range(XR)]
        ln_bn = sem("ln_bn")
        ln_mv = sem("ln_mv")
        ln_rstd = sem("ln_rstd")
        ln_eps = sem("ln_eps")
        xn_normed = sem("xn_normed")
        xn_hi_done = sem("xn_hi_done")
        xn_ready = sem("xn_ready")
        chain_done = sem("chain_done")
        hi_done = sem("hi_done")
        lo_done = sem("lo_done")
        tb_done = sem("tb_done")
        tb_hi = sem("tb_hi")
        tb_lo = sem("tb_lo")
        max_done = sem("max_done")
        exp_done = sem("exp_done")
        rec_done = sem("rec_done")
        a_hi_done = sem("a_hi_done")
        a_done = sem("a_done")
        y_done = sem("y_done")
        y_bn = sem("y_bn")
        y_mv = sem("y_mv")
        y_eps = sem("y_eps")
        y_rstd = sem("y_rstd")
        y_mr = sem("y_mr")
        y_free = sem("y_free")
        y_normed = sem("y_normed")
        x1_ready = sem("x1_ready")

        block = ctx.enter_context(nc.Block())

        @block.sync
        def _(sp):
            def load_x(b, t):
                if not (isinstance(b, int) and b == 0 and t < XR):
                    sp.wait_ge(xn_normed, b * NT + t + 1 - XR)
                sp.dma_start(x_in[:, t % XR, :], x_t[b * NT + t]).then_inc(x_loaded[t % XR], 16)

            def load_res(b, t):
                if not (isinstance(b, int) and b == 0 and t < XR):
                    sp.wait_ge(x1_stored[t % XR], (b * (NT // XR) + t // XR) * 16)
                sp.dma_start(x_res[:, t % XR, :], x_t[b * NT + t]).then_inc(res_loaded[t % XR], 16)

            def load_w(n, w):
                if n >= 2:
                    sp.wait_ge(w_lo_done, n - 1)
                sp.dma_start(w_stage[:, n % 2], w.rearrange("(k p) e -> p k e", p=P)).then_inc(w_loaded[n % 2], 16)

            def body(b, more):
                if more:
                    for t in range(NT):
                        load_x(b + 1, t)
                for t in range(NT):
                    sp.wait_ge(x1_ready, b * NT + t + 1)
                    sp.dma_start(x1_t[b * NT + t], x_res[:, t % XR, :]).then_inc(x1_stored[t % XR], 16)
                    if t + XR < NT:
                        load_res(b, t + XR)
                    elif more:
                        load_res(b + 1, t + XR - NT)

            for t in range(XR):
                load_x(0, t)
            load_w(0, wk)
            load_w(1, wq)
            for t in range(XR, NT):
                load_x(0, t)
            load_w(2, wo)
            load_w(3, wvT)
            for t in range(XR):
                load_res(0, t)
            with sp.Fori(0, B - 1) as b:
                body(b, True)
            body(B - 1, False)
            for q in range(XR):
                sp.wait_ge(x1_stored[q], B * (NT // XR) * 16)

        @block.gpsimd
        def _(pool):
            pool.memset(mhalf[:], -0.5).then_inc(s_ident, 1)
            pool.memset(eps[:], EPS).then_inc(s_ident, 1)
            pool.memset(ident32[:], 0.0).then_inc(s_ident, 1)
            pool.wait_ge(s_ident, 3)
            pool.affine_select(out=ident32[:], in_=ident32[:], compare_op=ALU.not_equal, fill=1.0,
                               base=0, pattern=[[-1, P]], channel_multiplier=1).then_inc(s_ident, 1)
            pool.wait_ge(s_ident, 4)
            pool.tensor_copy(ident16[:], ident32[:]).then_inc(s_ident, 1)

            def ln_scale(b, t):
                n = held(pool, b * NT + t + 1)
                pool.wait_ge(ln_mv, n)
                pool.tensor_tensor(rstd[:, t, 0:1], mv[:, t, 1:2], eps[:], ALU.add).then_inc(ln_eps, 1)
                pool.wait_ge(ln_eps, n)
                pool.tensor_tensor(rstd[:, t, 1:2], rstd[:, t, 0:1], mhalf[:], ALU.pow).then_inc(ln_rstd, 1)

            def y_scale(b, t):
                n = held(pool, b * NT + t + 1)
                pool.wait_ge(y_mv, n)
                pool.tensor_tensor(yr[:, t, 0:1], ymv[:, t, 1:2], eps[:], ALU.add).then_inc(y_eps, 1)
                pool.wait_ge(y_eps, n)
                pool.tensor_tensor(yr[:, t, 1:2], yr[:, t, 0:1], mhalf[:], ALU.pow).then_inc(y_rstd, 1)
                pool.wait_ge(y_rstd, n)
                pool.tensor_tensor(yr[:, t, 2:3], ymv[:, t, 0:1], yr[:, t, 1:2], ALU.mult).then_inc(y_mr, 1)

            def body(b, more):
                if more:
                    for t in range(NT):
                        ln_scale(b + 1, t)
                for t in range(NT):
                    y_scale(b, t)

            for t in range(NT):
                ln_scale(0, t)
            with pool.Fori(0, B - 1) as b:
                body(b, True)
            body(B - 1, False)

        @block.scalar
        def _(act):
            def ln_hi(b, t):
                act.wait_ge(xn_normed, b * NT + t + 1)
                if not (isinstance(b, int) and b == 0):
                    act.wait_ge(tb_done, b * TB)
                act.activation(xn_hi[:, t, :], xn[:, t % 2, :], ACT.Copy, scale=XN_SCALE).then_inc(xn_hi_done, 1)

            def evac_hi(b, n, stage, m, dst, lo, scale):
                act.wait_ge(chain_done, b * CHAIN + stage * K + m + 1)
                act.activation(dst[:, m, lo:E], chain[:, m, 0:E - lo], ACT.Copy, scale=scale).then_inc(hi_done, 1)

            def mirror_hi(b, m):
                act.wait_ge(tb_done, b * TB + m + 1)
                act.copy(ga_hi[:, m + 1:K, m * P:(m + 1) * P],
                         tbank[:, 0, 0:(K - 1 - m) * P].rearrange("p (c n) -> p c n", n=P)).then_inc(tb_hi, 1)

            def body(b, more):
                for m in range(K):
                    evac_hi(b, 0, 0, m, ga_hi, m * P, G_SCALE)
                    if m:
                        mirror_hi(b, m - 1)
                for m in range(K):
                    evac_hi(b, 1, 1, m, tu_hi, 0, 1.0)
                    act.wait_ge(tb_done, b * TB + K + m)
                    act.copy(xT_hi[:, m, :], tbank[:, 0, :].bitcast(F16)).then_inc(tb_hi, 1)
                for m in range(K):
                    act.wait_ge(max_done, b * K + m + 1)
                    if m >= 2:
                        act.wait_ge(a_done, b * K + m - 1)
                    act.activation(expd[:, m % 2, :], chain[:, m, :], ACT.Exp, bias=smax[:, m:m + 1],
                                   accum_out=ssum[:, m:m + 1]).then_inc(exp_done, 1)
                for s, dst, scale in ((3, tu_hi, 1.0), (4, m_hi, 1.0 / XN_SCALE)):
                    for m in range(K):
                        evac_hi(b, s - 1, s, m, dst, 0, scale)
                        t = (s - 3) * K + m - 1
                        if more and t >= 0:
                            ln_hi(b + 1, t)
                if more:
                    ln_hi(b + 1, NT - 1)
                for t in range(NT):
                    act.wait_ge(y_rstd, b * NT + t + 1)
                    if t >= 2:
                        act.wait_ge(x1_ready, b * NT + t - 1)
                    act.activation(y_n[:, t % 2, :], ybank[:, t % 2, :], ACT.Copy,
                                   scale=yr[:, t, 1:2]).then_inc(y_normed, 1)

            def weight_hi(n):
                act.wait_ge(w_loaded[n % 2], 16 * (n // 2 + 1))
                act.copy(w_hi[:, n], w_stage[:, n % 2]).then_inc(w_hi_done, 1)

            for t in range(NT):
                ln_hi(0, t)
            for n in range(4):
                weight_hi(n)
            with act.Fori(0, B - 1) as b:
                body(b, True)
            body(B - 1, False)

        @block.vector
        def _(dve):
            def ln_stats(b, t):
                n = held(dve, b * NT + t + 1)
                dve.wait_ge(x_loaded[t % XR], (b * (NT // XR) + t // XR + 1) * 16)
                dve.bn_stats(stats[:, t % 2, :], x_in[:, t % XR, :]).then_inc(ln_bn, 1)
                dve.wait_ge(ln_bn, n)
                dve.memset(carrier[:], 0.0)
                dve.bn_aggr(mv[:, t, :], stats[:, t % 2, :]).then_inc(ln_mv, 1)

            def ln_norm(b, t):
                n = held(dve, b * NT + t + 1)
                dve.wait_ge(ln_rstd, n)
                if not (isinstance(b, int) and b == 0 and t < 2):
                    dve.wait_ge(xn_ready, n - 2)
                dve.tensor_scalar(xn[:, t % 2, :], x_in[:, t % XR, :], mv[:, t, 0:1], rstd[:, t, 1:2],
                                  ALU.subtract, ALU.mult).then_inc(xn_normed, 1)

            def ln_lo(b, t):
                dve.wait_ge(xn_hi_done, b * NT + t + 1)
                dve.scalar_tensor_tensor(out=xn_lo[:, t, :], in0=xn[:, t % 2, :], scalar=XN_SCALE, in1=xn_hi[:, t, :],
                                         op0=ALU.mult, op1=ALU.subtract).then_inc(xn_ready, 1)

            def ln_step(b, j):
                if j < NT:
                    ln_stats(b, j)
                if 1 <= j <= NT:
                    ln_norm(b, j - 1)
                if 2 <= j:
                    ln_lo(b, j - 2)

            def evac_lo(b, n, m, hi, lo_t, lo, scale):
                dve.wait_ge(hi_done, b * EVACS + n * K + m + 1)
                dve.scalar_tensor_tensor(out=lo_t[:, m, lo:E], in0=chain[:, m, 0:E - lo], scalar=scale,
                                         in1=f32(hi[:, m, lo:E]), op0=ALU.mult, op1=ALU.subtract).then_inc(lo_done, 1)

            def mirror_lo(b, m):
                dve.wait_ge(tb_done, b * TB + m + 1)
                dve.tensor_copy(ga_lo[:, m + 1:K, m * P:(m + 1) * P],
                                tbank[:, 1, 0:(K - 1 - m) * P].rearrange("p (c n) -> p c n", n=P)).then_inc(tb_lo, 1)

            def body(b, more):
                for m in range(K):
                    evac_lo(b, 0, m, ga_hi, ga_lo, m * P, G_SCALE)
                    if m:
                        mirror_lo(b, m - 1)
                for m in range(K):
                    evac_lo(b, 1, m, tu_hi, tu_lo, 0, 1.0)
                    dve.wait_ge(tb_done, b * TB + K + m)
                    dve.tensor_copy(xT_lo[:, m, :], tbank[:, 1, :].bitcast(F16)).then_inc(tb_lo, 1)
                for m in range(K + 1):
                    if m < K:
                        dve.wait_ge(chain_done, b * CHAIN + 2 * K + m + 1)
                        dve.tensor_reduce(smax[:, m:m + 1], chain[:, m, :], AX.X, ALU.max,
                                          negate=True).then_inc(max_done, 1)
                    if m >= 1:
                        e = expd[:, (m - 1) % 2, :]
                        dve.wait_ge(exp_done, b * K + m)
                        dve.reciprocal(srec[:, m - 1:m], ssum[:, m - 1:m]).then_inc(rec_done, 1)
                        dve.wait_ge(rec_done, b * K + m)
                        dve.tensor_scalar(ga_hi[:, m - 1, :], e, srec[:, m - 1:m], None,
                                          ALU.mult).then_inc(a_hi_done, 1)
                        dve.wait_ge(a_hi_done, b * K + m)
                        dve.scalar_tensor_tensor(out=ga_lo[:, m - 1, :], in0=e, scalar=srec[:, m - 1:m],
                                                 in1=f32(ga_hi[:, m - 1, :]), op0=ALU.mult,
                                                 op1=ALU.subtract).then_inc(a_done, 1)
                for s, hi, lo_t, scale in ((2, tu_hi, tu_lo, 1.0), (3, m_hi, m_lo, 1.0 / XN_SCALE)):
                    for m in range(K):
                        evac_lo(b, s, m, hi, lo_t, 0, scale)
                        if more:
                            ln_step(b + 1, (s - 2) * K + m)
                if more:
                    ln_step(b + 1, NT)
                    ln_step(b + 1, NT + 1)

                for t in range(NT + 1):
                    if t < NT:
                        n = held(dve, b * NT + t + 1)
                        dve.wait_ge(y_done, n)
                        dve.bn_stats(ystats[:, t % 2, :], ybank[:, t % 2, :]).then_inc(y_bn, 1)
                        dve.wait_ge(y_bn, n)
                        dve.memset(carrier[:], 0.0)
                        dve.bn_aggr(ymv[:, t, :], ystats[:, t % 2, :]).then_inc(y_mv, 1)
                    if t >= 1:
                        u = t - 1
                        dve.wait_ge(y_normed, b * NT + t)
                        dve.wait_ge(res_loaded[u % XR], (b * (NT // XR) + u // XR + 1) * 16)
                        dve.wait_ge(y_mr, b * NT + t)
                        dve.scalar_tensor_tensor(out=x_res[:, u % XR, :], in0=y_n[:, u % 2, :],
                                                 scalar=yr[:, u, 2:3], in1=x_res[:, u % XR, :],
                                                 op0=ALU.subtract, op1=ALU.add).then_inc(x1_ready, 1)

            def weight_lo(n):
                dve.wait_ge(w_hi_done, n + 1)
                dve.tensor_tensor(w_lo[:, n], w_stage[:, n % 2], f32(w_hi[:, n]), ALU.subtract).then_inc(w_lo_done, 1)

            for j in range(NT + 2):
                ln_step(0, j)
            for n in range(4):
                weight_lo(n)
            with dve.Fori(0, B - 1) as b:
                body(b, True)
            body(B - 1, False)

        @block.tensor
        def _(pe):
            def product(out, l_hi, l_lo, r_hi, r_lo, start, stop):
                pe.matmul(out, l_hi, r_hi, start=start, stop=False)
                pe.matmul(out, l_hi, r_lo, start=False, stop=False)
                return pe.matmul(out, l_lo, r_hi, start=False, stop=stop)

            def mirror(b, m):
                pe.wait_ge(lo_done, b * EVACS + m + 1)
                if m:
                    pe.wait_ge(tb_hi, b * TB + m)
                    pe.wait_ge(tb_lo, b * TB + m)
                for part, src in ((0, ga_hi), (1, ga_lo)):
                    for c in range(m + 1, K):
                        mm = pe.transpose(tbank[:, part, (c - m - 1) * P:(c - m) * P],
                                          f32(src[:, m, c * P:(c + 1) * P]), ident32[:])
                mm.then_inc(tb_done, 1)

            def gram(b, m):
                for t in range(NT):
                    if m == 0:
                        pe.wait_ge(xn_ready, b * NT + t + 1)
                    c = slice(m * P, (m + 1) * P)
                    mm = product(chain[:, m, 0:E - m * P], xn_hi[:, t, c], xn_lo[:, t, c],
                                 xn_hi[:, t, m * P:E], xn_lo[:, t, m * P:E], t == 0, t == NT - 1)
                mm.then_inc(chain_done, 1)

            def square(m, hi, lo, r_hi, r_lo, ready):
                for k in range(K):
                    if ready:
                        ready(k)
                    c = slice(m * P, (m + 1) * P)
                    mm = product(chain[:, m, :], hi(k)[:, c], lo(k)[:, c], r_hi(k), r_lo(k), k == 0, k == K - 1)
                mm.then_inc(chain_done, 1)

            def tile_of(t):
                return lambda k: t[:, k, :]

            def weight(t, w):
                return lambda k: t[:, w, k, :]

            def body(b):
                for m in range(K):
                    gram(b, m)
                    if m:
                        mirror(b, m - 1)
                for m in range(K):
                    if m < K - 1:
                        pe.wait_ge(tb_hi, b * TB + m + 1)
                        pe.wait_ge(tb_lo, b * TB + m + 1)
                    else:
                        pe.wait_ge(lo_done, b * EVACS + K)
                    if isinstance(b, int) or True:
                        pe.wait_ge(w_lo_done, WK + 1)
                    square(m, tile_of(ga_hi), tile_of(ga_lo), weight(w_hi, WK), weight(w_lo, WK), None)
                    u = K - 1 + m
                    pe.wait_ge(tb_hi, b * TB + u)
                    pe.wait_ge(tb_lo, b * TB + u)
                    for part, src in ((0, xn_hi), (1, xn_lo)):
                        for t in range(NT):
                            mm = pe.transpose(tbank[:, part, :].bitcast(F16)[:, t * P:(t + 1) * P],
                                              src[:, t, m * P:(m + 1) * P], ident16[:])
                    mm.then_inc(tb_done, 1)
                pe.wait_ge(w_lo_done, WQ + 1)
                for m in range(K):
                    square(m, weight(w_hi, WQ), weight(w_lo, WQ), tile_of(tu_hi), tile_of(tu_lo),
                           (lambda k: pe.wait_ge(lo_done, b * EVACS + K + k + 1)) if m == 0 else None)
                pe.wait_ge(w_lo_done, WO + 1)
                for m in range(K):
                    square(m, tile_of(ga_hi), tile_of(ga_lo), weight(w_hi, WO), weight(w_lo, WO),
                           (lambda k: pe.wait_ge(a_done, b * K + k + 1)) if m == 0 else None)
                pe.wait_ge(w_lo_done, WV + 1)
                for m in range(K):
                    square(m, weight(w_hi, WV), weight(w_lo, WV), tile_of(tu_hi), tile_of(tu_lo),
                           (lambda k: pe.wait_ge(lo_done, b * EVACS + 2 * K + k + 1)) if m == 0 else None)
                pe.wait_ge(tb_hi, b * TB + TB)
                pe.wait_ge(tb_lo, b * TB + TB)
                for t in range(NT):
                    if t >= 2:
                        pe.wait_ge(y_normed, b * NT + t - 1)
                    c = slice(t * P, (t + 1) * P)
                    for k in range(K):
                        if t == 0:
                            pe.wait_ge(lo_done, b * EVACS + 3 * K + k + 1)
                        mm = product(ybank[:, t % 2, :], xT_hi[:, k, c], xT_lo[:, k, c], m_hi[:, k, :],
                                     m_lo[:, k, :], k == 0, k == K - 1)
                    mm.then_inc(y_done, 1)

            pe.wait_ge(s_ident, 5)
            with pe.Fori(0, B - 1) as b:
                body(b)
            body(B - 1)


G_SCALE = XN_SCALE ** -2 * 0.25


def power_of_two(n):
    return 2.0 ** n


def weights_block(nc, control, basis, later_half, vander, wt_hi, wt_lo, c_gate, c_up, c_out):
    COLS = basis.shape[2] * 4
    CHUNK = COLS // 4
    UNITS = COLS // BANK
    PIECES = CHUNK // BANK
    GATE, UP, DOWN = range(3)

    with ExitStack() as ctx:
        def sb(name, shape, dt):
            return ctx.enter_context(nc.sbuf_tensor(name, shape, dt))

        def psum(name, shape, dt):
            return ctx.enter_context(nc.psum_tensor(name, shape, dt))

        def sem(name):
            return ctx.enter_context(nc.semaphore(name))

        ctrl = sb("ctrl", [P, 3, CHUNK], F32)
        coef = sb("coef", [P, 2, CHUNK], F32)
        half = sb("half", [P, 2, COLS], mybir.dt.uint8)
        vand = sb("vand", [P, 2, P], F32)
        wt = sb("wt", [P, 2, BANK], F32)
        cmax = sb("cmax", [P, 3], F32)
        call = sb("call", [P, 3], F32)
        expo = sb("expo", [P, 3], F32)
        rexpo = sb("rexpo", [P, 3], F32)
        wscale = sb("wscale", [P, 3], F32)
        c_gu = sb("c_gu", [P, 1], F32)

        bank = [psum(f"wbank{i}", [P, BANK], F32) for i in range(8)]

        vand_loaded = sem("vand_loaded")
        ctrl_loaded = [sem(f"ctrl_loaded{i}") for i in range(3)]
        coef_loaded = [sem(f"coef_loaded{i}") for i in range(2)]
        half_loaded = [sem(f"half_loaded{i}") for i in range(2)]
        max_part = sem("max_part")
        max_all = sem("max_all")
        scale_step = sem("scale_step")
        prod_done = sem("prod_done")
        piece_done = sem("piece_done")
        first_copied = sem("first_copied")
        second_merged = sem("second_merged")
        wt_hi_done = sem("wt_hi_done")
        wt_done = sem("wt_done")

        block = ctx.enter_context(nc.Block())

        @block.sync
        def _(sp):
            sp.dma_start(ctrl[:, 0, :], control[0]).then_inc(ctrl_loaded[0], 16)
            sp.dma_start(coef[:, 0, :], basis[0]).then_inc(coef_loaded[0], 16)
            sp.dma_start(vand[:], vander).then_inc(vand_loaded, 16)
            sp.dma_start(half[:, 0, :], later_half[0].bitcast(mybir.dt.uint8)).then_inc(half_loaded[0], 16)
            sp.dma_start(ctrl[:, 1, :], control[1]).then_inc(ctrl_loaded[1], 16)
            sp.dma_start(ctrl[:, 2, :], control[2]).then_inc(ctrl_loaded[2], 16)
            sp.dma_start(coef[:, 1, :], basis[1]).then_inc(coef_loaded[1], 16)
            sp.dma_start(half[:, 1, :], later_half[1].bitcast(mybir.dt.uint8)).then_inc(half_loaded[1], 16)

        @block.gpsimd
        def _(pool):
            pool.wait_ge(max_part, 3)
            pool.partition_all_reduce(call[:], cmax[:], P, bass.bass_isa.ReduceOp.max).then_inc(max_all, 1)

        @block.scalar
        def _(act):
            def wt_hi_part(w, n):
                act.wait_ge(second_merged, w * UNITS + n + 1)
                c = (n % 4) * PIECES + n // 4
                act.copy(wt_hi[:, w, c, :], wt[:, n % 2, :]).then_inc(wt_hi_done, 1)

            def weights(w, first):
                for n in range(UNITS):
                    act.wait_ge(piece_done, w * UNITS + n + 1)
                    if not (first and n < 2):
                        act.wait_ge(wt_done, w * UNITS + n - 1)
                    act.copy(wt[:, n % 2, :], bank[n % 4][:]).then_inc(first_copied, 1)
                    if n >= 1:
                        wt_hi_part(w, n - 1)
                wt_hi_part(w, UNITS - 1)

            weights(0, True)
            with act.Fori(1, 3) as w:
                weights(w, False)

        @block.vector
        def _(dve):
            for w in range(3):
                dve.wait_ge(ctrl_loaded[w], 16)
                dve.tensor_reduce(cmax[:, w:w + 1], ctrl[:, w, :], AX.X, ALU.max,
                                  apply_absolute_value=True).then_inc(max_part, 1)
            U32 = mybir.dt.uint32
            dve.wait_ge(max_all, 1)
            dve.tensor_scalar(cmax[:], call[:], power_of_two(-60), None, ALU.max).then_inc(scale_step, 1)
            dve.wait_ge(scale_step, 1)
            dve.tensor_scalar(expo[:].bitcast(U32), cmax[:].bitcast(U32), 0x7F800000, None,
                              ALU.bitwise_and).then_inc(scale_step, 1)
            dve.wait_ge(scale_step, 2)
            dve.reciprocal(rexpo[:], expo[:]).then_inc(scale_step, 1)
            dve.tensor_scalar(c_gate[:], expo[:, GATE:GATE + 1], power_of_two(-24), None,
                              ALU.mult).then_inc(scale_step, 1)
            dve.tensor_tensor(c_gu[:], expo[:, GATE:GATE + 1], expo[:, UP:UP + 1], ALU.mult).then_inc(scale_step, 1)
            dve.wait_ge(scale_step, 5)
            dve.tensor_scalar(wscale[:], rexpo[:], power_of_two(13), None, ALU.mult).then_inc(scale_step, 1)
            dve.tensor_scalar(c_up[:], rexpo[:, GATE:GATE + 1], power_of_two(-29), None,
                              ALU.mult).then_inc(scale_step, 1)
            dve.tensor_scalar(c_out[:], c_gu[:], expo[:, DOWN:DOWN + 1], power_of_two(-8),
                              ALU.mult, ALU.mult).then_inc(scale_step, 1)
            dve.wait_ge(scale_step, 8)
            for w in range(3):
                if w in (GATE, DOWN):
                    dve.wait_ge(coef_loaded[w // 2], 16)
                dve.scalar_tensor_tensor(out=ctrl[:, w, :], in0=ctrl[:, w, :], scalar=wscale[:, w:w + 1],
                                         in1=coef[:, w // 2, :], op0=ALU.mult, op1=ALU.mult).then_inc(prod_done, 1)

            def wt_lo_part(w, n):
                dve.wait_ge(wt_hi_done, w * UNITS + n + 1)
                c = (n % 4) * PIECES + n // 4
                dve.tensor_tensor(wt_lo[:, w, c, :], wt[:, n % 2, :], wt_hi[:, w, c, :], ALU.subtract).then_inc(wt_done, 1)

            def weights(w, kind):
                for n in range(UNITS):
                    c = (n % 4) * PIECES + n // 4
                    dve.wait_ge(first_copied, w * UNITS + n + 1)
                    dve.copy_predicated(wt[:, n % 2, :], half[:, kind, c * BANK:(c + 1) * BANK],
                                        bank[4 + n % 4][:]).then_inc(second_merged, 1)
                    if n >= 1:
                        wt_lo_part(w, n - 1)
                wt_lo_part(w, UNITS - 1)

            dve.wait_ge(half_loaded[0], 16)
            for w in (GATE, UP):
                weights(w, 0)
            dve.wait_ge(half_loaded[1], 16)
            weights(DOWN, 1)

        @block.tensor
        def _(pe):
            pe.wait_ge(vand_loaded, 16)

            def weights(w, first):
                for n in range(UNITS):
                    rows = slice(32 * (n % 4), 32 * (n % 4) + 32)
                    cols = slice(n // 4 * BANK, (n // 4 + 1) * BANK)
                    if not (first and n < 4):
                        pe.wait_ge(second_merged, w * UNITS + n - 3)
                    pe.matmul(bank[n % 4][:], vand[rows, 0, :], ctrl[rows, w, cols], start=True, stop=True)
                    pe.matmul(bank[4 + n % 4][:], vand[rows, 1, :], ctrl[rows, w, cols], start=True,
                              stop=True).then_inc(piece_done, 1)

            for w in range(3):
                pe.wait_ge(prod_done, w + 1)
                weights(w, w == 0)


def ffn_block(nc, x1, wt_hi, wt_lo, c_gate, c_up, c_out, out):
    N, E = x1.shape
    K = E // P
    TOK = 512
    Q = TOK // P
    GROUPS = N // TOK
    I = wt_hi.shape[2]
    GATE, UP, DOWN = range(3)
    FIRST, LAST4 = 2, I - 4
    x1_t = x1.rearrange("(n p) e -> n p e", p=P)
    out_t = out.rearrange("(n p) e -> n p e", p=P)

    with ExitStack() as ctx:
        def sb(name, shape, dt):
            return ctx.enter_context(nc.sbuf_tensor(name, shape, dt))

        def psum(name, shape, dt):
            return ctx.enter_context(nc.psum_tensor(name, shape, dt))

        def sem(name):
            return ctx.enter_context(nc.semaphore(name))

        x1_in = sb("x1_in", [P, 2, Q, E], F32)
        hn = sb("hn", [P, 2, E], F32)
        h_hi = sb("h_hi", [P, Q, E], F16)
        h_lo = sb("h_lo", [P, Q, E], F16)
        hT = sb("hT", [P, 2, 2, K, TOK], F16)
        gated = sb("gated", [P, 2, TOK], F32)
        inter = sb("inter", [P, 2, TOK], F32)
        inter_hi = sb("inter_hi", [P, 2, TOK], F16)
        inter_lo = sb("inter_lo", [P, 2, TOK], F16)
        y = sb("y", [P, Q, E], F32)
        id32 = sb("id32", [P, P], F32)
        id16 = sb("id16", [P, P], F16)
        hstats = sb("hstats", [P, 2, 6], F32)
        hmv = sb("hmv", [P, Q, 2], F32)
        hr = sb("hr", [P, Q, 2], F32)
        ostats = sb("ostats", [P, 2, 6], F32)
        omv = sb("omv", [P, Q, 2], F32)
        orr = sb("orr", [P, Q, 2], F32)
        mhalf2 = sb("mhalf2", [P, 1], F32)
        eps2 = sb("eps2", [P, 1], F32)
        carrier2 = sb("carrier2", [P, 1], F32)

        bank = [psum(f"bank{i}", [P, BANK], F32) for i in range(8)]
        gbank, ubank, tb, dbank = bank[0], bank[1], bank[2:4], bank[4:8]

        c_ready = sem("c_ready")
        x1_loaded = [[sem(f"x1_loaded{p}{q}") for q in range(Q)] for p in range(2)]
        out_stored = [[sem(f"out_stored{p}{q}") for q in range(Q)] for p in range(2)]
        h_bn = sem("h_bn")
        h_mv = sem("h_mv")
        h_eps = sem("h_eps")
        h_rstd = sem("h_rstd")
        h_normed = sem("h_normed")
        h_hi_done = sem("h_hi_done")
        h_ready = sem("h_ready")
        hT_done = sem("hT_done")
        hT_copied = sem("hT_copied")
        gate_done = sem("gate_done")
        up_done = sem("up_done")
        silu_done = sem("silu_done")
        inter_done = sem("inter_done")
        inter_hi_done = sem("inter_hi_done")
        inter_ready = sem("inter_ready")
        down_done = sem("down_done")
        y_copied = sem("y_copied")
        o_bn = sem("o_bn")
        o_mv = sem("o_mv")
        o_eps = sem("o_eps")
        o_rstd = sem("o_rstd")
        o_normed = sem("o_normed")
        out_ready = sem("out_ready")

        block = ctx.enter_context(nc.Block())

        def groups(engine, group):
            with engine.Fori(0, GROUPS // 2 - 1) as pair:
                group(2 * pair, 0, True)
                group(2 * pair + 1, 1, True)
            group(GROUPS - 2, 0, True)
            group(GROUPS - 1, 1, False)

        def steps(engine, g, par, more, step):
            for i in range(FIRST):
                step(g, par, i, i, more)
            with engine.Fori(0, (LAST4 - FIRST) // 2) as j:
                for s in range(2):
                    step(g, par, FIRST + 2 * j + s, FIRST + s, more)
            for i in range(LAST4, I):
                step(g, par, i, i, more)

        @block.sync
        def _(sp):
            for g in range(2):
                for q in range(Q):
                    sp.dma_start(x1_in[:, g, q, :], x1_t[g * Q + q]).then_inc(x1_loaded[g][q], 16)

            def store(g, par, count, load):
                for q in range(Q):
                    sp.wait_ge(out_ready, g * Q + q + 1)
                    sp.dma_start(out_t[g * Q + q], x1_in[:, par, q, :]).then_inc(out_stored[par][q], 16)
                if load:
                    for q in range(Q):
                        sp.wait_ge(out_stored[par][q], count * 16)
                        sp.dma_start(x1_in[:, par, q, :], x1_t[(g + 2) * Q + q]).then_inc(x1_loaded[par][q], 16)

            with sp.Fori(0, GROUPS // 2 - 1) as pair:
                for par in range(2):
                    store(2 * pair + par, par, pair + 1, True)
            for par in range(2):
                store(GROUPS - 2 + par, par, GROUPS // 2, False)
            for par in range(2):
                for q in range(Q):
                    sp.wait_ge(out_stored[par][q], GROUPS // 2 * 16)

        @block.gpsimd
        def _(pool):
            pool.memset(mhalf2[:], -0.5).then_inc(c_ready, 1)
            pool.memset(eps2[:], EPS).then_inc(c_ready, 1)
            pool.memset(id32[:], 0.0).then_inc(c_ready, 1)
            pool.wait_ge(c_ready, 3)
            pool.affine_select(out=id32[:], in_=id32[:], compare_op=ALU.not_equal, fill=1.0,
                               base=0, pattern=[[-1, P]], channel_multiplier=1).then_inc(c_ready, 1)
            pool.wait_ge(c_ready, 4)
            pool.tensor_copy(id16[:], id32[:]).then_inc(c_ready, 1)
            def h_scale(g, q):
                n = held(pool, g * Q + q + 1)
                pool.wait_ge(h_mv, n)
                pool.tensor_tensor(hr[:, q, 0:1], hmv[:, q, 1:2], eps2[:], ALU.add).then_inc(h_eps, 1)
                pool.wait_ge(h_eps, n)
                pool.tensor_tensor(hr[:, q, 1:2], hr[:, q, 0:1], mhalf2[:], ALU.pow).then_inc(h_rstd, 1)

            def o_scale(g, q):
                n = held(pool, g * Q + q + 1)
                pool.wait_ge(o_mv, n)
                pool.tensor_tensor(orr[:, q, 0:1], omv[:, q, 1:2], eps2[:], ALU.add).then_inc(o_eps, 1)
                pool.wait_ge(o_eps, n)
                pool.tensor_tensor(orr[:, q, 1:2], orr[:, q, 0:1], mhalf2[:], ALU.pow).then_inc(o_rstd, 1)

            for q in range(Q):
                h_scale(0, q)
            for q in range(Q):
                h_scale(1, q)
            with pool.Fori(0, GROUPS - 2) as g:
                for q in range(Q):
                    o_scale(g, q)
                for q in range(Q):
                    h_scale(g + 2, q)
            for g in range(GROUPS - 2, GROUPS):
                for q in range(Q):
                    o_scale(g, q)

        @block.scalar
        def _(act):
            act.sem_inc(y_copied, Q)

            def h_hi_part(g, q):
                act.wait_ge(h_normed, g * Q + q + 1)
                act.activation(h_hi[:, q, :], hn[:, q % 2, :], ACT.Copy, scale=XN_SCALE).then_inc(h_hi_done, 1)

            def evac(n, par):
                act.wait_ge(gate_done, n + 1)
                act.activation(gated[:, par, :], gbank[:], ACT.Silu, scale=c_gate[:]).then_inc(silu_done, 1)
                act.wait_ge(inter_done, n + 1)
                if not (isinstance(n, int) and n == 0):
                    act.wait_ge(down_done, n)
                act.copy(inter_hi[:, par, :], inter[:, par, :]).then_inc(inter_hi_done, 1)

            def step(g, par, i, i_static, more):
                if more or i_static < I - 1:
                    evac(g * I + i + 1, (i_static + 1) % 2)
                if more and LAST4 <= i_static < LAST4 + 2:
                    for q in range(2 * (i_static - LAST4), 2 * (i_static - LAST4) + 2):
                        h_hi_part(g + 1, q)
                if i_static == I - 1:
                    for q in range(Q):
                        act.wait_ge(down_done, (g + 1) * I + 1)
                        act.activation(y[:, q, :], dbank[q][:], ACT.Copy, scale=c_out[:]).then_inc(y_copied, 1)

            for q in range(Q):
                h_hi_part(0, q)
            evac(0, 0)
            groups(act, lambda g, par, more: steps(act, g, par, more, step))

        @block.vector
        def _(dve):
            def h_norm(g, q, par, count):
                n = held(dve, g * Q + q + 1)
                x = x1_in[:, par, q, :]
                dve.wait_ge(x1_loaded[par][q], count * 16)
                dve.bn_stats(hstats[:, q % 2, :], x).then_inc(h_bn, 1)
                dve.wait_ge(h_bn, n)
                dve.memset(carrier2[:], 0.0)
                dve.bn_aggr(hmv[:, q, :], hstats[:, q % 2, :]).then_inc(h_mv, 1)
                dve.wait_ge(h_rstd, n)
                dve.tensor_scalar(hn[:, q % 2, :], x, hmv[:, q, 0:1], hr[:, q, 1:2],
                                  ALU.subtract, ALU.mult).then_inc(h_normed, 1)
                dve.wait_ge(h_hi_done, n)
                dve.scalar_tensor_tensor(out=h_lo[:, q, :], in0=hn[:, q % 2, :], scalar=XN_SCALE,
                                         in1=h_hi[:, q, :], op0=ALU.mult, op1=ALU.subtract).then_inc(h_ready, 1)

            def hT_copy(g, par, q):
                dve.wait_ge(hT_done, g * Q + q + 1)
                dve.tensor_copy(hT[:, par, :, :, q * P:(q + 1) * P].rearrange("p a k n -> p (a k) n"),
                                tb[q % 2][:].bitcast(F16).rearrange("p (a n) -> p a n", n=P)).then_inc(hT_copied, 1)

            def evac(n, par):
                dve.wait_ge(silu_done, n + 1)
                dve.wait_ge(up_done, n + 1)
                dve.scalar_tensor_tensor(out=inter[:, par, :], in0=ubank[:], scalar=c_up[:],
                                         in1=gated[:, par, :], op0=ALU.mult, op1=ALU.mult).then_inc(inter_done, 1)
                dve.wait_ge(inter_hi_done, n + 1)
                dve.tensor_tensor(inter_lo[:, par, :], inter[:, par, :], inter_hi[:, par, :],
                                  ALU.subtract).then_inc(inter_ready, 1)

            def finish(g, par, q):
                n = held(dve, g * Q + q + 1)
                dve.wait_ge(y_copied, n + Q)
                dve.bn_stats(ostats[:, q % 2, :], y[:, q, :]).then_inc(o_bn, 1)
                dve.wait_ge(o_bn, n)
                dve.memset(carrier2[:], 0.0)
                dve.bn_aggr(omv[:, q, :], ostats[:, q % 2, :]).then_inc(o_mv, 1)
                dve.wait_ge(o_rstd, n)
                dve.tensor_scalar(y[:, q, :], y[:, q, :], omv[:, q, 0:1], orr[:, q, 1:2],
                                  ALU.subtract, ALU.mult).then_inc(o_normed, 1)
                dve.wait_ge(o_normed, n)
                dve.tensor_tensor(x1_in[:, par, q, :], y[:, q, :], x1_in[:, par, q, :], ALU.add).then_inc(out_ready, 1)

            def group(g, par, more, count, first):
                def step(g, par, i, i_static, more):
                    if more and i_static == LAST4 + 2:
                        for q in range(Q):
                            hT_copy(g + 1, 1 - par, q)
                    if more or i_static < I - 1:
                        evac(g * I + i + 1, (i_static + 1) % 2)
                    if i_static < 2 and not first:
                        for q in range(2 * i_static, 2 * i_static + 2):
                            finish(g - 1, 1 - par, q)
                    if more and LAST4 <= i_static < LAST4 + 2:
                        for q in range(2 * (i_static - LAST4), 2 * (i_static - LAST4) + 2):
                            h_norm(g + 1, q, 1 - par, count)
                steps(dve, g, par, more, step)

            for q in range(Q):
                h_norm(0, q, 0, 1)
            for q in range(Q):
                hT_copy(0, 0, q)
            evac(0, 0)
            group(0, 0, True, 1, True)
            with dve.Fori(0, GROUPS // 2 - 1) as pair:
                group(2 * pair + 1, 1, True, pair + 2, False)
                group(2 * pair + 2, 0, True, pair + 2, False)
            group(GROUPS - 1, 1, False, 0, False)
            for q in range(Q):
                finish(GROUPS - 1, 1, q)

        @block.tensor
        def _(pe):
            pe.sem_inc(down_done, 1)
            pe.wait_ge(c_ready, 5)

            def product(out, l_hi, l_lo, r_hi, r_lo, start, stop):
                pe.matmul(out, l_hi, r_hi, start=start, stop=False)
                pe.matmul(out, l_hi, r_lo, start=False, stop=False)
                return pe.matmul(out, l_lo, r_hi, start=False, stop=stop)

            def turn(g, q):
                pe.wait_ge(h_ready, g * Q + q + 1)
                if q >= 2:
                    pe.wait_ge(hT_copied, g * Q + q - 1)
                view = tb[q % 2][:].bitcast(F16)
                for part, src in ((0, h_hi), (1, h_lo)):
                    for k in range(K):
                        mm = pe.transpose(view[:, (part * K + k) * P:(part * K + k + 1) * P],
                                          src[:, q, k * P:(k + 1) * P], id16[:])
                mm.then_inc(hT_done, 1)

            def gate_up(g, par, i, first):
                n = g * I + i
                for w, dst, free, done in ((GATE, gbank, silu_done, gate_done), (UP, ubank, inter_done, up_done)):
                    if not first:
                        pe.wait_ge(free, n)
                    for k in range(K):
                        c = slice(k * P, (k + 1) * P)
                        mm = product(dst[:], wt_hi[:, w, i, c], wt_lo[:, w, i, c], hT[:, par, 0, k, :],
                                     hT[:, par, 1, k, :], k == 0, k == K - 1)
                    mm.then_inc(done, 1)

            def down(g, i, i_static):
                pe.wait_ge(inter_ready, g * I + i + 1)
                s = i_static % 2
                for q in range(Q):
                    if i_static == 0:
                        pe.wait_ge(y_copied, g * Q + q + 1)
                    c = slice(q * P, (q + 1) * P)
                    mm = product(dbank[q][:], inter_hi[:, s, c], inter_lo[:, s, c], wt_hi[:, DOWN, i, :],
                                 wt_lo[:, DOWN, i, :], i_static == 0, i_static == I - 1)
                mm.then_inc(down_done, 1)

            def step(g, par, i, i_static, more):
                if more and i_static == LAST4 + 2:
                    for q in range(Q):
                        turn(g + 1, q)
                if i_static < I - 1:
                    gate_up(g, par, i + 1, False)
                elif more:
                    pe.wait_ge(hT_copied, (g + 2) * Q)
                    gate_up(g + 1, 1 - par, 0, False)
                down(g, i, i_static)

            for q in range(Q):
                turn(0, q)
            pe.wait_ge(hT_copied, Q)
            gate_up(0, 0, 0, True)
            groups(pe, lambda g, par, more: steps(pe, g, par, more, step))


def spline_tables(rows_of_column, n_ctrl, n_samples):
    import numpy as np
    step = (n_ctrl - 1.0) / (n_samples - 1)
    r = np.asarray(rows_of_column)
    seg = np.minimum(np.floor(step * P * r).astype(np.int64), n_ctrl - 2)
    catmull = 0.5 * np.array([[0, 2, 0, 0], [-1, 0, 1, 0], [2, -5, 4, -1], [-1, 3, -3, 1]], np.float64)
    binom = np.array([[1, 0, 0, 0], [1, 1, 0, 0], [1, 2, 1, 0], [1, 3, 3, 1]], np.float64)
    points = np.empty((32, r.size), np.int64)
    coef = np.empty((32, r.size), np.float64)
    half = P // 2
    for later in range(2):
        mid = step * (P * r + half) - seg - later
        for m in range(4):
            for q in range(4):
                row = 16 * later + 4 * m + q
                points[row] = np.clip(seg + later + q - 1, 0, n_ctrl - 1)
                coef[row] = sum(catmull[j, q] * binom[j, m] * mid ** (j - m) for j in range(m, 4)) * (step * half) ** m
    n = P * r[None, :] + np.arange(P)[:, None]
    at = np.minimum(np.floor(step * n).astype(np.int64), n_ctrl - 2)
    assert ((at - seg) >= 0).all() and ((at - seg) <= 1).all()
    fold = lambda a: np.concatenate(np.split(a, 4, axis=1), axis=0)
    return fold(points), fold(coef).astype(np.float32), (at > seg).astype(np.uint8)


def vandermonde():
    import numpy as np
    v = (np.arange(P) - P // 2) / (P // 2)
    table = np.zeros((P, 2, P), np.float32)
    for g in range(4):
        for later in range(2):
            for m in range(4):
                for q in range(4):
                    table[32 * g + 16 * later + 4 * m + q, later] = v ** m
    return table


def build(nc, x, wq, wk, wvT, wo, control, basis, later_half, vander, out):
    x1 = nc.dram_tensor("x1", out.shape, F32, kind="Internal").ap()
    attention_block(nc, x, wq, wk, wvT, wo, x1)
    K, I = x.shape[2] // P, 4 * x.shape[2] // P
    with ExitStack() as ctx:
        def sb(name, shape, dt):
            return ctx.enter_context(nc.sbuf_tensor(name, shape, dt))

        wt_hi = sb("wt_hi", [P, 3, I, K * P], F16)
        wt_lo = sb("wt_lo", [P, 3, I, K * P], F16)
        c_gate = sb("c_gate", [P, 1], F32)
        c_up = sb("c_up", [P, 1], F32)
        c_out = sb("c_out", [P, 1], F32)
        weights_block(nc, control, basis, later_half, vander, wt_hi, wt_lo, c_gate, c_up, c_out)
        ffn_block(nc, x1, wt_hi, wt_lo, c_gate, c_up, c_out, out)


def kernel(**inputs):
    import numpy as np
    import concourse.bacc as bacc
    from concourse.bass_utils import run_bass_kernel_spmd as run

    nc = bacc.Bacc("TRN2", target_bir_lowering=False, num_devices=1)
    arrays = {}

    def dram(name, a):
        arrays[name] = np.ascontiguousarray(a)
        return nc.dram_tensor(name, arrays[name].shape, mybir.dt.from_np(arrays[name].dtype), kind="ExternalInput").ap()

    x = np.asarray(inputs["L0_attn_x"])
    hidden = x.shape[-1]
    cps = [np.asarray(inputs[f"L0_ffn_{n}_cp"]) for n in ("gate", "up", "down")]
    n_ctrl = cps[0].shape[0]
    ffn = 4 * hidden
    K, I = hidden // P, ffn // P
    i, k, c = np.meshgrid(np.arange(I), np.arange(K), np.arange(P), indexing="ij")
    rows_in = (K * (P * i + c) + k).ravel()
    i, h = np.meshgrid(np.arange(I), np.arange(hidden), indexing="ij")
    rows_out = (I * h + i).ravel()
    tables = [spline_tables(rows, n_ctrl, ffn * hidden) for rows in (rows_in, rows_out)]
    control = np.stack([cps[0][tables[0][0]], cps[1][tables[0][0]], cps[2][tables[1][0]]])
    args = [
        dram("x", x), dram("wq", inputs["L0_attn_Wq"]), dram("wk", inputs["L0_attn_Wk"]),
        dram("wvT", np.asarray(inputs["L0_attn_Wv"]).T), dram("wo", inputs["L0_attn_Wo"]),
        dram("control", control), dram("basis", np.stack([t[1] for t in tables])),
        dram("later_half", np.stack([t[2] for t in tables]).view(np.int32)), dram("vander", vandermonde()),
    ]
    out = nc.dram_tensor("out", (x.shape[0] * x.shape[1], hidden), F32, kind="ExternalOutput").ap()
    build(nc, *args, out)
    result = run(nc, [arrays], core_ids=[0])
    return result.results[0]["out"].reshape(x.shape)
```

```python
from contextlib import ExitStack

import concourse.bass as bass
from concourse import mybir

ALU = mybir.AluOpType
ACT = mybir.ActivationFunctionType
AX = mybir.AxisListType
F32 = mybir.dt.float32
F32R = mybir.dt.float32r
F16 = mybir.dt.float16

P = 128
EPS = 1e-5
XN_SCALE = 2.0 ** 11
BANK = 512


def f32(ap):
    return ap.bitcast(F32)


def held(engine, value):
    return value if isinstance(value, int) else engine.snap(value)


def attention_block(nc, x, wq, wk, wvT, wo, x1):
    B, S, E = x.shape
    K = E // P
    NT = S // P
    XR = 4
    CHAIN, EVACS, TB = 5 * K, 4 * K, K - 1 + K
    SELF = 2 * NT
    x_t = x.rearrange("b (t p) e -> (b t) p e", p=P)
    x1_t = x1.rearrange("(n p) e -> n p e", p=P)

    with ExitStack() as ctx:
        def sb(name, shape, dt):
            return ctx.enter_context(nc.sbuf_tensor(name, shape, dt))

        def psum(name, shape, dt):
            return ctx.enter_context(nc.psum_tensor(name, shape, dt))

        def sem(name):
            return ctx.enter_context(nc.semaphore(name))

        WK, WQ, WO, WV = range(4)
        w_stage = sb("w_stage", [P, 2, K, E], F32)
        w_hi = sb("w_hi", [P, 4, K, E], F32R)
        w_lo = sb("w_lo", [P, 4, K, E], F32R)
        x_in = sb("x_in", [P, XR, E], F32)
        xn = sb("xn", [P, 2, E], F32)
        xn_hi = sb("xn_hi", [P, NT, E], F16)
        xn_lo = sb("xn_lo", [P, NT, E], F16)
        xT_hi = sb("xT_hi", [P, K, S], F32R)
        xT_lo = sb("xT_lo", [P, K, S], F32R)
        ga_hi = sb("ga_hi", [P, K, E], F32R)
        ga_lo = sb("ga_lo", [P, K, E], F32R)
        tu_hi = sb("tu_hi", [P, K, E], F32R)
        tu_lo = sb("tu_lo", [P, K, E], F32R)
        m_hi = sb("m_hi", [P, K, E], F32R)
        m_lo = sb("m_lo", [P, K, E], F32R)
        expd = sb("expd", [P, 2, E], F32)
        x_res = sb("x_res", [P, XR, E], F32)
        y_n = sb("y_n", [P, 2, E], F32)
        ident32 = sb("ident32", [P, P], F32)
        ident16 = sb("ident16", [P, P], F16)
        stats = sb("stats", [P, 2, 6], F32)
        mv = sb("mv", [P, NT, 2], F32)
        rstd = sb("rstd", [P, NT, 2], F32)
        ystats = sb("ystats", [P, 2, 6], F32)
        ymv = sb("ymv", [P, NT, 2], F32)
        yr = sb("yr", [P, NT, 3], F32)
        smax = sb("smax", [P, K], F32)
        ssum = sb("ssum", [P, K], F32)
        srec = sb("srec", [P, K], F32)
        mhalf = sb("mhalf", [P, 1], F32)
        eps = sb("eps", [P, 1], F32)
        carrier = sb("carrier", [P, 1], F32)

        chain = psum("chain", [P, K, BANK], F32)
        ybank = psum("ybank", [P, 2, BANK], F32)
        tbank = psum("tbank", [P, 2, BANK], F32)

        s_ident = sem("s_ident")
        w_loaded = [sem(f"w_loaded{i}") for i in range(2)]
        w_hi_done = sem("w_hi_done")
        w_lo_done = sem("w_lo_done")
        x_loaded = [sem(f"x_loaded{i}") for i in range(XR)]
        res_loaded = [sem(f"res_loaded{i}") for i in range(XR)]
        x1_stored = [sem(f"x1_stored{i}") for i in range(XR)]
        ln_bn = sem("ln_bn")
        ln_mv = sem("ln_mv")
        ln_rstd = sem("ln_rstd")
        ln_eps = sem("ln_eps")
        xn_normed = sem("xn_normed")
        xn_hi_done = sem("xn_hi_done")
        xn_ready = sem("xn_ready")
        chain_done = sem("chain_done")
        hi_done = sem("hi_done")
        lo_done = sem("lo_done")
        tb_done = sem("tb_done")
        tb_hi = sem("tb_hi")
        tb_lo = sem("tb_lo")
        max_done = sem("max_done")
        exp_done = sem("exp_done")
        rec_done = sem("rec_done")
        a_hi_done = sem("a_hi_done")
        a_done = sem("a_done")
        y_done = sem("y_done")
        y_bn = sem("y_bn")
        y_mv = sem("y_mv")
        y_eps = sem("y_eps")
        y_rstd = sem("y_rstd")
        y_mr = sem("y_mr")
        y_free = sem("y_free")
        y_normed = sem("y_normed")
        x1_ready = sem("x1_ready")

        block = ctx.enter_context(nc.Block())

        @block.sync
        def _(sp):
            def load_x(b, t):
                if not (isinstance(b, int) and b == 0 and t < XR):
                    sp.wait_ge(xn_normed, b * NT + t + 1 - XR)
                sp.dma_start(x_in[:, t % XR, :], x_t[b * NT + t]).then_inc(x_loaded[t % XR], 16)

            def load_res(b, t):
                if not (isinstance(b, int) and b == 0 and t < XR):
                    sp.wait_ge(x1_stored[t % XR], (b * (NT // XR) + t // XR) * 16)
                sp.dma_start(x_res[:, t % XR, :], x_t[b * NT + t]).then_inc(res_loaded[t % XR], 16)

            def load_w(n, w):
                if n >= 2:
                    sp.wait_ge(w_lo_done, n - 1)
                sp.dma_start(w_stage[:, n % 2], w.rearrange("(k p) e -> p k e", p=P)).then_inc(w_loaded[n % 2], 16)

            def body(b, more):
                if more:
                    for t in range(NT):
                        load_x(b + 1, t)
                for t in range(NT):
                    sp.wait_ge(x1_ready, b * NT + t + 1)
                    sp.dma_start(x1_t[b * NT + t], x_res[:, t % XR, :]).then_inc(x1_stored[t % XR], 16)
                    if t + XR < NT:
                        load_res(b, t + XR)
                    elif more:
                        load_res(b + 1, t + XR - NT)

            for t in range(XR):
                load_x(0, t)
            load_w(0, wk)
            load_w(1, wq)
            for t in range(XR, NT):
                load_x(0, t)
            load_w(2, wo)
            load_w(3, wvT)
            for t in range(XR):
                load_res(0, t)
            with sp.Fori(0, B - 1) as b:
                body(b, True)
            body(B - 1, False)
            for q in range(XR):
                sp.wait_ge(x1_stored[q], B * (NT // XR) * 16)

        @block.gpsimd
        def _(pool):
            pool.memset(mhalf[:], -0.5).then_inc(s_ident, 1)
            pool.memset(eps[:], EPS).then_inc(s_ident, 1)
            pool.memset(ident32[:], 0.0).then_inc(s_ident, 1)
            pool.wait_ge(s_ident, 3)
            pool.affine_select(out=ident32[:], in_=ident32[:], compare_op=ALU.not_equal, fill=1.0,
                               base=0, pattern=[[-1, P]], channel_multiplier=1).then_inc(s_ident, 1)
            pool.wait_ge(s_ident, 4)
            pool.tensor_copy(ident16[:], ident32[:]).then_inc(s_ident, 1)

            def ln_scale(b, t):
                n = held(pool, b * NT + t + 1)
                pool.wait_ge(ln_mv, n)
                pool.tensor_tensor(rstd[:, t, 0:1], mv[:, t, 1:2], eps[:], ALU.add).then_inc(ln_eps, 1)
                pool.wait_ge(ln_eps, n)
                pool.tensor_tensor(rstd[:, t, 1:2], rstd[:, t, 0:1], mhalf[:], ALU.pow).then_inc(ln_rstd, 1)

            def y_scale(b, t):
                n = held(pool, b * NT + t + 1)
                pool.wait_ge(y_mv, n)
                pool.tensor_tensor(yr[:, t, 0:1], ymv[:, t, 1:2], eps[:], ALU.add).then_inc(y_eps, 1)
                pool.wait_ge(y_eps, n)
                pool.tensor_tensor(yr[:, t, 1:2], yr[:, t, 0:1], mhalf[:], ALU.pow).then_inc(y_rstd, 1)
                pool.wait_ge(y_rstd, n)
                pool.tensor_tensor(yr[:, t, 2:3], ymv[:, t, 0:1], yr[:, t, 1:2], ALU.mult).then_inc(y_mr, 1)

            def body(b, more):
                if more:
                    for t in range(NT):
                        ln_scale(b + 1, t)
                for t in range(NT):
                    y_scale(b, t)

            for t in range(NT):
                ln_scale(0, t)
            with pool.Fori(0, B - 1) as b:
                body(b, True)
            body(B - 1, False)

        @block.scalar
        def _(act):
            def ln_hi(b, t):
                act.wait_ge(xn_normed, b * NT + t + 1)
                if not (isinstance(b, int) and b == 0):
                    act.wait_ge(tb_done, b * TB)
                act.activation(xn_hi[:, t, :], xn[:, t % 2, :], ACT.Copy, scale=XN_SCALE).then_inc(xn_hi_done, 1)

            def evac_hi(b, n, stage, m, dst, lo, scale):
                act.wait_ge(chain_done, b * CHAIN + stage * K + m + 1)
                act.activation(dst[:, m, lo:E], chain[:, m, 0:E - lo], ACT.Copy, scale=scale).then_inc(hi_done, 1)

            def mirror_hi(b, m):
                act.wait_ge(tb_done, b * TB + m + 1)
                act.copy(ga_hi[:, m + 1:K, m * P:(m + 1) * P],
                         tbank[:, 0, 0:(K - 1 - m) * P].rearrange("p (c n) -> p c n", n=P)).then_inc(tb_hi, 1)

            def body(b, more):
                for m in range(K):
                    evac_hi(b, 0, 0, m, ga_hi, m * P, G_SCALE)
                    if m:
                        mirror_hi(b, m - 1)
                for m in range(K):
                    evac_hi(b, 1, 1, m, tu_hi, 0, 1.0)
                    act.wait_ge(tb_done, b * TB + K + m)
                    act.copy(xT_hi[:, m, :], tbank[:, 0, :].bitcast(F16)).then_inc(tb_hi, 1)
                for m in range(K):
                    act.wait_ge(max_done, b * K + m + 1)
                    if m >= 2:
                        act.wait_ge(a_done, b * K + m - 1)
                    act.activation(expd[:, m % 2, :], chain[:, m, :], ACT.Exp, bias=smax[:, m:m + 1],
                                   accum_out=ssum[:, m:m + 1]).then_inc(exp_done, 1)
                for s, dst, scale in ((3, tu_hi, 1.0), (4, m_hi, 1.0 / XN_SCALE)):
                    for m in range(K):
                        evac_hi(b, s - 1, s, m, dst, 0, scale)
                        t = (s - 3) * K + m - 1
                        if more and t >= 0:
                            ln_hi(b + 1, t)
                if more:
                    ln_hi(b + 1, NT - 1)
                for t in range(NT):
                    act.wait_ge(y_rstd, b * NT + t + 1)
                    if t >= 2:
                        act.wait_ge(x1_ready, b * NT + t - 1)
                    act.activation(y_n[:, t % 2, :], ybank[:, t % 2, :], ACT.Copy,
                                   scale=yr[:, t, 1:2]).then_inc(y_normed, 1)

            def weight_hi(n):
                act.wait_ge(w_loaded[n % 2], 16 * (n // 2 + 1))
                act.copy(w_hi[:, n], w_stage[:, n % 2]).then_inc(w_hi_done, 1)

            for t in range(NT):
                ln_hi(0, t)
            for n in range(4):
                weight_hi(n)
            with act.Fori(0, B - 1) as b:
                body(b, True)
            body(B - 1, False)

        @block.vector
        def _(dve):
            def ln_stats(b, t):
                n = held(dve, b * NT + t + 1)
                dve.wait_ge(x_loaded[t % XR], (b * (NT // XR) + t // XR + 1) * 16)
                dve.bn_stats(stats[:, t % 2, :], x_in[:, t % XR, :]).then_inc(ln_bn, 1)
                dve.wait_ge(ln_bn, n)
                dve.memset(carrier[:], 0.0)
                dve.bn_aggr(mv[:, t, :], stats[:, t % 2, :]).then_inc(ln_mv, 1)

            def ln_norm(b, t):
                n = held(dve, b * NT + t + 1)
                dve.wait_ge(ln_rstd, n)
                if not (isinstance(b, int) and b == 0 and t < 2):
                    dve.wait_ge(xn_ready, n - 2)
                dve.tensor_scalar(xn[:, t % 2, :], x_in[:, t % XR, :], mv[:, t, 0:1], rstd[:, t, 1:2],
                                  ALU.subtract, ALU.mult).then_inc(xn_normed, 1)

            def ln_lo(b, t):
                dve.wait_ge(xn_hi_done, b * NT + t + 1)
                dve.scalar_tensor_tensor(out=xn_lo[:, t, :], in0=xn[:, t % 2, :], scalar=XN_SCALE, in1=xn_hi[:, t, :],
                                         op0=ALU.mult, op1=ALU.subtract).then_inc(xn_ready, 1)

            def ln_step(b, j):
                if j < NT:
                    ln_stats(b, j)
                if 1 <= j <= NT:
                    ln_norm(b, j - 1)
                if 2 <= j:
                    ln_lo(b, j - 2)

            def evac_lo(b, n, m, hi, lo_t, lo, scale):
                dve.wait_ge(hi_done, b * EVACS + n * K + m + 1)
                dve.scalar_tensor_tensor(out=lo_t[:, m, lo:E], in0=chain[:, m, 0:E - lo], scalar=scale,
                                         in1=f32(hi[:, m, lo:E]), op0=ALU.mult, op1=ALU.subtract).then_inc(lo_done, 1)

            def mirror_lo(b, m):
                dve.wait_ge(tb_done, b * TB + m + 1)
                dve.tensor_copy(ga_lo[:, m + 1:K, m * P:(m + 1) * P],
                                tbank[:, 1, 0:(K - 1 - m) * P].rearrange("p (c n) -> p c n", n=P)).then_inc(tb_lo, 1)

            def body(b, more):
                for m in range(K):
                    evac_lo(b, 0, m, ga_hi, ga_lo, m * P, G_SCALE)
                    if m:
                        mirror_lo(b, m - 1)
                for m in range(K):
                    evac_lo(b, 1, m, tu_hi, tu_lo, 0, 1.0)
                    dve.wait_ge(tb_done, b * TB + K + m)
                    dve.tensor_copy(xT_lo[:, m, :], tbank[:, 1, :].bitcast(F16)).then_inc(tb_lo, 1)
                for m in range(K + 1):
                    if m < K:
                        dve.wait_ge(chain_done, b * CHAIN + 2 * K + m + 1)
                        dve.tensor_reduce(smax[:, m:m + 1], chain[:, m, :], AX.X, ALU.max,
                                          negate=True).then_inc(max_done, 1)
                    if m >= 1:
                        e = expd[:, (m - 1) % 2, :]
                        dve.wait_ge(exp_done, b * K + m)
                        dve.reciprocal(srec[:, m - 1:m], ssum[:, m - 1:m]).then_inc(rec_done, 1)
                        dve.wait_ge(rec_done, b * K + m)
                        dve.tensor_scalar(ga_hi[:, m - 1, :], e, srec[:, m - 1:m], None,
                                          ALU.mult).then_inc(a_hi_done, 1)
                        dve.wait_ge(a_hi_done, b * K + m)
                        dve.scalar_tensor_tensor(out=ga_lo[:, m - 1, :], in0=e, scalar=srec[:, m - 1:m],
                                                 in1=f32(ga_hi[:, m - 1, :]), op0=ALU.mult,
                                                 op1=ALU.subtract).then_inc(a_done, 1)
                for s, hi, lo_t, scale in ((2, tu_hi, tu_lo, 1.0), (3, m_hi, m_lo, 1.0 / XN_SCALE)):
                    for m in range(K):
                        evac_lo(b, s, m, hi, lo_t, 0, scale)
                        if more:
                            ln_step(b + 1, (s - 2) * K + m)
                if more:
                    ln_step(b + 1, NT)
                    ln_step(b + 1, NT + 1)

                for t in range(NT + 1):
                    if t < NT:
                        n = held(dve, b * NT + t + 1)
                        dve.wait_ge(y_done, n)
                        dve.bn_stats(ystats[:, t % 2, :], ybank[:, t % 2, :]).then_inc(y_bn, 1)
                        dve.wait_ge(y_bn, n)
                        dve.memset(carrier[:], 0.0)
                        dve.bn_aggr(ymv[:, t, :], ystats[:, t % 2, :]).then_inc(y_mv, 1)
                    if t >= 1:
                        u = t - 1
                        dve.wait_ge(y_normed, b * NT + t)
                        dve.wait_ge(res_loaded[u % XR], (b * (NT // XR) + u // XR + 1) * 16)
                        dve.wait_ge(y_mr, b * NT + t)
                        dve.scalar_tensor_tensor(out=x_res[:, u % XR, :], in0=y_n[:, u % 2, :],
                                                 scalar=yr[:, u, 2:3], in1=x_res[:, u % XR, :],
                                                 op0=ALU.subtract, op1=ALU.add).then_inc(x1_ready, 1)

            def weight_lo(n):
                dve.wait_ge(w_hi_done, n + 1)
                dve.tensor_tensor(w_lo[:, n], w_stage[:, n % 2], f32(w_hi[:, n]), ALU.subtract).then_inc(w_lo_done, 1)

            for j in range(NT + 2):
                ln_step(0, j)
            for n in range(4):
                weight_lo(n)
            with dve.Fori(0, B - 1) as b:
                body(b, True)
            body(B - 1, False)

        @block.tensor
        def _(pe):
            def product(out, l_hi, l_lo, r_hi, r_lo, start, stop):
                pe.matmul(out, l_hi, r_hi, start=start, stop=False)
                pe.matmul(out, l_hi, r_lo, start=False, stop=False)
                return pe.matmul(out, l_lo, r_hi, start=False, stop=stop)

            def mirror(b, m):
                pe.wait_ge(lo_done, b * EVACS + m + 1)
                if m:
                    pe.wait_ge(tb_hi, b * TB + m)
                    pe.wait_ge(tb_lo, b * TB + m)
                for part, src in ((0, ga_hi), (1, ga_lo)):
                    for c in range(m + 1, K):
                        mm = pe.transpose(tbank[:, part, (c - m - 1) * P:(c - m) * P],
                                          f32(src[:, m, c * P:(c + 1) * P]), ident32[:])
                mm.then_inc(tb_done, 1)

            def gram(b, m):
                for t in range(NT):
                    if m == 0:
                        pe.wait_ge(xn_ready, b * NT + t + 1)
                    c = slice(m * P, (m + 1) * P)
                    mm = product(chain[:, m, 0:E - m * P], xn_hi[:, t, c], xn_lo[:, t, c],
                                 xn_hi[:, t, m * P:E], xn_lo[:, t, m * P:E], t == 0, t == NT - 1)
                mm.then_inc(chain_done, 1)

            def square(m, hi, lo, r_hi, r_lo, ready):
                for k in range(K):
                    if ready:
                        ready(k)
                    c = slice(m * P, (m + 1) * P)
                    mm = product(chain[:, m, :], hi(k)[:, c], lo(k)[:, c], r_hi(k), r_lo(k), k == 0, k == K - 1)
                mm.then_inc(chain_done, 1)

            def tile_of(t):
                return lambda k: t[:, k, :]

            def weight(t, w):
                return lambda k: t[:, w, k, :]

            def body(b):
                for m in range(K):
                    gram(b, m)
                    if m:
                        mirror(b, m - 1)
                for m in range(K):
                    if m < K - 1:
                        pe.wait_ge(tb_hi, b * TB + m + 1)
                        pe.wait_ge(tb_lo, b * TB + m + 1)
                    else:
                        pe.wait_ge(lo_done, b * EVACS + K)
                    if isinstance(b, int) or True:
                        pe.wait_ge(w_lo_done, WK + 1)
                    square(m, tile_of(ga_hi), tile_of(ga_lo), weight(w_hi, WK), weight(w_lo, WK), None)
                    u = K - 1 + m
                    pe.wait_ge(tb_hi, b * TB + u)
                    pe.wait_ge(tb_lo, b * TB + u)
                    for part, src in ((0, xn_hi), (1, xn_lo)):
                        for t in range(NT):
                            mm = pe.transpose(tbank[:, part, :].bitcast(F16)[:, t * P:(t + 1) * P],
                                              src[:, t, m * P:(m + 1) * P], ident16[:])
                    mm.then_inc(tb_done, 1)
                pe.wait_ge(w_lo_done, WQ + 1)
                for m in range(K):
                    square(m, weight(w_hi, WQ), weight(w_lo, WQ), tile_of(tu_hi), tile_of(tu_lo),
                           (lambda k: pe.wait_ge(lo_done, b * EVACS + K + k + 1)) if m == 0 else None)
                pe.wait_ge(w_lo_done, WO + 1)
                for m in range(K):
                    square(m, tile_of(ga_hi), tile_of(ga_lo), weight(w_hi, WO), weight(w_lo, WO),
                           (lambda k: pe.wait_ge(a_done, b * K + k + 1)) if m == 0 else None)
                pe.wait_ge(w_lo_done, WV + 1)
                for m in range(K):
                    square(m, weight(w_hi, WV), weight(w_lo, WV), tile_of(tu_hi), tile_of(tu_lo),
                           (lambda k: pe.wait_ge(lo_done, b * EVACS + 2 * K + k + 1)) if m == 0 else None)
                pe.wait_ge(tb_hi, b * TB + TB)
                pe.wait_ge(tb_lo, b * TB + TB)
                for t in range(NT):
                    if t >= 2:
                        pe.wait_ge(y_normed, b * NT + t - 1)
                    c = slice(t * P, (t + 1) * P)
                    for k in range(K):
                        if t == 0:
                            pe.wait_ge(lo_done, b * EVACS + 3 * K + k + 1)
                        mm = product(ybank[:, t % 2, :], xT_hi[:, k, c], xT_lo[:, k, c], m_hi[:, k, :],
                                     m_lo[:, k, :], k == 0, k == K - 1)
                    mm.then_inc(y_done, 1)

            pe.wait_ge(s_ident, 5)
            with pe.Fori(0, B - 1) as b:
                body(b)
            body(B - 1)


G_SCALE = XN_SCALE ** -2 * 0.25


WINDOW = 8
FEATURES = 8 + WINDOW
FEATURE_SCALE = 2.0 ** 8
Z_SCALE = 2.0 ** 7


def power_of_two(n):
    return 2.0 ** n


def weights_block(nc, raw_ctrl, unit_ctrl, unit_coef, row_ctrl, row_coef, later_half, vander,
                  s_dram, d_dram, c_gate, c_up, c_out):
    GATE, UP, DOWN = range(3)
    ROWS, UNITS_IN_HALF = unit_coef.shape[0], unit_coef.shape[2]
    KF = ROWS // 2
    TILES = later_half.shape[1] * 4 // BANK
    PIECES = TILES // 4
    STAGES = 4

    with ExitStack() as ctx:
        def sb(name, shape, dt):
            return ctx.enter_context(nc.sbuf_tensor(name, shape, dt))

        def psum(name, shape, dt):
            return ctx.enter_context(nc.psum_tensor(name, shape, dt))

        def sem(name):
            return ctx.enter_context(nc.semaphore(name))

        raw = sb("raw", list(raw_ctrl.shape), F32)
        units = sb("units", [P, 2, 5, UNITS_IN_HALF], F32)
        ucoef = sb("ucoef", [P, 5, UNITS_IN_HALF], F32)
        s_hi = sb("s_hi", [P, 2, UNITS_IN_HALF], F16)
        s_lo = sb("s_lo", [P, 2, UNITS_IN_HALF], F16)
        rows_in = sb("rows_in", [P, PIECES * BANK], F32)
        rcoef = sb("rcoef", [P, PIECES * BANK], F32)
        half = sb("half", [P, TILES * BANK], mybir.dt.uint8)
        vand = sb("vand", [P, 2, P], F32)
        dense = sb("dense", [P, 2, BANK], F32)
        split = sb("split", [P, STAGES, 2, BANK], F16)
        cmax = sb("cmax", [P, 3], F32)
        call = sb("call", [P, 3], F32)
        expo = sb("expo", [P, 3], F32)
        rexpo = sb("rexpo", [P, 3], F32)
        wscale = sb("wscale", [P, 3], F32)
        c_gu = sb("c_gu", [P, 1], F32)

        first_bank = [psum(f"first_bank{i}", [P, BANK], F32) for i in range(4)]
        second_bank = [psum(f"second_bank{i}", [P, BANK], F32) for i in range(4)]

        raw_loaded = sem("raw_loaded")
        rows_loaded = sem("rows_loaded")
        vand_loaded = sem("vand_loaded")
        half_loaded = sem("half_loaded")
        ucoef_loaded = sem("ucoef_loaded")
        units_loaded = [sem(f"units_loaded{w}") for w in range(2)]
        max_part = sem("max_part")
        max_all = sem("max_all")
        scale_step = sem("scale_step")
        rows_ready = sem("rows_ready")
        sum_step = [sem(f"sum_step{w}") for w in range(2)]
        s_hi_done = sem("s_hi_done")
        s_ready = sem("s_ready")
        s_stored = sem("s_stored")
        pieces_done = sem("pieces_done")
        first_copied = sem("first_copied")
        second_merged = sem("second_merged")
        d_hi_done = sem("d_hi_done")
        d_ready = sem("d_ready")
        d_stored = [sem(f"d_stored{i}") for i in range(STAGES)]

        block = ctx.enter_context(nc.Block())

        @block.sync
        def _(sp):
            sp.dma_start(raw[:], raw_ctrl).then_inc(raw_loaded, 16)
            sp.dma_start(rows_in[:], row_ctrl).then_inc(rows_loaded, 16)
            sp.dma_start(rcoef[:], row_coef).then_inc(rows_loaded, 16)
            sp.dma_start(vand[:], vander).then_inc(vand_loaded, 16)
            sp.dma_start(half[:], later_half.bitcast(mybir.dt.uint8)).then_inc(half_loaded, 16)
            sp.dma_start(ucoef[:], unit_coef).then_inc(ucoef_loaded, 16)
            for w in (UP, GATE):
                sp.dma_start(units[:, w], unit_ctrl[w]).then_inc(units_loaded[w], 16)
            for t in range(TILES):
                sp.wait_ge(d_ready, t + 1)
                sp.dma_start(d_dram[t], split[:, t % STAGES]).then_inc(d_stored[t % STAGES], 16)
            for n in range(2):
                w = (GATE, UP)[n]
                sp.wait_ge(s_ready, n + 1)
                for part in range(2):
                    rows = slice(part * KF, (part + 1) * KF)
                    cols = slice(part * UNITS_IN_HALF, (part + 1) * UNITS_IN_HALF)
                    sp.dma_start(s_dram[0, :, w, cols], s_hi[rows, w]).then_inc(s_stored, 16)
                    sp.dma_start(s_dram[1, :, w, cols], s_lo[rows, w]).then_inc(s_stored, 16)
            sp.wait_ge(s_stored, 8 * 16)
            for i in range(STAGES):
                sp.wait_ge(d_stored[i], TILES // STAGES * 16)

        def sums(engine, w):
            engine.wait_ge(ucoef_loaded, 16)
            engine.wait_ge(units_loaded[w], 16)
            engine.tensor_tensor(units[:, w], units[:, w], ucoef[:], ALU.mult).then_inc(sum_step[w], 1)
            engine.wait_ge(sum_step[w], 1)
            engine.tensor_tensor(units[:, w, 0:2], units[:, w, 0:2], units[:, w, 2:4], ALU.add).then_inc(sum_step[w], 1)
            engine.wait_ge(sum_step[w], 2)
            engine.tensor_tensor(units[:, w, 0], units[:, w, 0], units[:, w, 1], ALU.add).then_inc(sum_step[w], 1)
            engine.wait_ge(sum_step[w], 3)
            engine.tensor_tensor(units[:, w, 0], units[:, w, 0], units[:, w, 4], ALU.add).then_inc(sum_step[w], 1)

        @block.gpsimd
        def _(pool):
            pool.wait_ge(max_part, 1)
            pool.partition_all_reduce(call[:], cmax[:], P, bass.bass_isa.ReduceOp.max).then_inc(max_all, 1)
            sums(pool, UP)

        @block.scalar
        def _(act):
            def d_hi(t):
                act.wait_ge(second_merged, t + 1)
                if t >= STAGES:
                    act.wait_ge(d_stored[t % STAGES], t // STAGES * 16)
                act.copy(split[:, t % STAGES, 0], dense[:, t % 2, :]).then_inc(d_hi_done, 1)

            for n in range(TILES):
                act.wait_ge(pieces_done, n + 1)
                if n >= 2:
                    act.wait_ge(d_ready, n - 1)
                act.copy(dense[:, n % 2, :], first_bank[n % 4][:]).then_inc(first_copied, 1)
                if n >= 1:
                    d_hi(n - 1)
            d_hi(TILES - 1)
            for w in (GATE, UP):
                act.wait_ge(sum_step[w], 4)
                act.activation(s_hi[:, w], units[:, w, 0], ACT.Copy, scale=wscale[:, w:w + 1]).then_inc(s_hi_done, 1)

        @block.vector
        def _(dve):
            U32 = mybir.dt.uint32
            dve.wait_ge(raw_loaded, 16)
            dve.tensor_reduce(cmax[:], raw[:], AX.X, ALU.max, apply_absolute_value=True).then_inc(max_part, 1)
            dve.wait_ge(max_all, 1)
            dve.tensor_scalar(cmax[:], call[:], power_of_two(-60), None, ALU.max).then_inc(scale_step, 1)
            dve.wait_ge(scale_step, 1)
            dve.tensor_scalar(expo[:].bitcast(U32), cmax[:].bitcast(U32), 0x7F800000, None,
                              ALU.bitwise_and).then_inc(scale_step, 1)
            dve.wait_ge(scale_step, 2)
            dve.reciprocal(rexpo[:], expo[:]).then_inc(scale_step, 1)
            dve.tensor_scalar(c_gate[:], expo[:, GATE:GATE + 1], power_of_two(-12) / Z_SCALE, None,
                              ALU.mult).then_inc(scale_step, 1)
            dve.tensor_tensor(c_gu[:], expo[:, GATE:GATE + 1], expo[:, UP:UP + 1], ALU.mult).then_inc(scale_step, 1)
            dve.wait_ge(scale_step, 5)
            dve.tensor_scalar(wscale[:, GATE:UP + 1], rexpo[:, GATE:UP + 1], power_of_two(12), None,
                              ALU.mult).then_inc(scale_step, 1)
            dve.tensor_scalar(wscale[:, DOWN:DOWN + 1], rexpo[:, DOWN:DOWN + 1], power_of_two(13), None,
                              ALU.mult).then_inc(scale_step, 1)
            dve.tensor_scalar(c_up[:], rexpo[:, GATE:GATE + 1], power_of_two(-17) / Z_SCALE, None,
                              ALU.mult).then_inc(scale_step, 1)
            dve.tensor_scalar(c_out[:], c_gu[:], expo[:, DOWN:DOWN + 1], power_of_two(-8),
                              ALU.mult, ALU.mult).then_inc(scale_step, 1)
            dve.wait_ge(scale_step, 9)
            dve.wait_ge(rows_loaded, 32)
            dve.scalar_tensor_tensor(out=rows_in[:], in0=rows_in[:], scalar=wscale[:, DOWN:DOWN + 1],
                                     in1=rcoef[:], op0=ALU.mult, op1=ALU.mult).then_inc(rows_ready, 1)

            def d_lo(t):
                dve.wait_ge(d_hi_done, t + 1)
                dve.tensor_tensor(split[:, t % STAGES, 1], dense[:, t % 2, :], split[:, t % STAGES, 0],
                                  ALU.subtract).then_inc(d_ready, 1)

            dve.wait_ge(half_loaded, 16)
            for n in range(TILES):
                dve.wait_ge(first_copied, n + 1)
                dve.copy_predicated(dense[:, n % 2, :], half[:, n * BANK:(n + 1) * BANK],
                                    second_bank[n % 4][:]).then_inc(second_merged, 1)
                if n >= 1:
                    d_lo(n - 1)
            d_lo(TILES - 1)
            sums(dve, GATE)
            for n in range(2):
                w = (GATE, UP)[n]
                dve.wait_ge(s_hi_done, n + 1)
                dve.scalar_tensor_tensor(out=s_lo[:, w], in0=units[:, w, 0], scalar=wscale[:, w:w + 1],
                                         in1=s_hi[:, w], op0=ALU.mult, op1=ALU.subtract).then_inc(s_ready, 1)

        @block.tensor
        def _(pe):
            pe.wait_ge(vand_loaded, 16)
            pe.wait_ge(rows_ready, 1)
            for n in range(TILES):
                rows = slice(32 * (n // PIECES), 32 * (n // PIECES) + 32)
                cols = slice(n % PIECES * BANK, (n % PIECES + 1) * BANK)
                if n >= 4:
                    pe.wait_ge(second_merged, n - 3)
                pe.matmul(first_bank[n % 4][:], vand[rows, 0, :], rows_in[rows, cols], start=True, stop=True)
                pe.matmul(second_bank[n % 4][:], vand[rows, 1, :], rows_in[rows, cols], start=True,
                          stop=True).then_inc(pieces_done, 1)


def ffn_block(nc, x1, features, perm, s_dram, d_dram, z_spill, c_gate, c_up, c_out, out):
    N, E = x1.shape
    K = E // P
    TOK = 512
    Q = TOK // P
    GROUPS = N // TOK
    I = perm.shape[1]
    HALF = I // 2
    UNITS = 2 * K
    KF = K * FEATURES
    ZCOLS = HALF * FEATURES
    STEPS = GROUPS * I
    GATE, UP = range(2)
    RING = 4
    x1_t = x1.rearrange("(n p) e -> n p e", p=P)
    out_t = out.rearrange("(n p) e -> n p e", p=P)

    with ExitStack() as ctx:
        def sb(name, shape, dt):
            return ctx.enter_context(nc.sbuf_tensor(name, shape, dt))

        def psum(name, shape, dt):
            return ctx.enter_context(nc.psum_tensor(name, shape, dt))

        def sem(name):
            return ctx.enter_context(nc.semaphore(name))

        x_ln = sb("x_ln", [P, RING, E], F32)
        x_res = sb("x_res2", [P, Q, E], F32)
        feat = sb("feat", [P, 2, K, I * FEATURES], F16)
        s_twice = sb("s_twice", [P, 2, I * P], F16)
        s_low = sb("s_low", [KF, 2, I * P], F16)
        wd = sb("wd", [P, I, 2 * E], F16)
        order = sb("order", [P, I], mybir.dt.int32)
        hn = sb("hn", [P, E], F32)
        h_hi = sb("h_hi", [P, E], F16)
        h_lo = sb("h_lo", [P, E], F16)
        hT = sb("hT", [P, 2, K, P], F16)
        z_hi = sb("z_hi", [P, UNITS, TOK], F16)
        z_lo = sb("z_lo", [P, UNITS, TOK], F16)
        z = [sb(f"z{par}", [P, I, TOK], F16) for par in range(2)]
        gated = sb("gated", [P, 2, TOK], F32)
        inter = sb("inter", [P, 2, TOK], F32)
        inter_hi = sb("inter_hi", [P, 4, TOK], F16)
        inter_lo = sb("inter_lo", [P, 4, TOK], F16)
        y = sb("y", [P, Q, E], F32)
        id32 = sb("id32", [P, P], F32)
        id16 = sb("id16", [P, P], F16)
        hstats = sb("hstats", [P, 6], F32)
        hmv = sb("hmv", [P, 2], F32)
        hr = sb("hr", [P, 2], F32)
        ostats = sb("ostats", [P, 2, 6], F32)
        omv = sb("omv", [P, Q, 2], F32)
        orr = sb("orr", [P, Q, 2], F32)
        mhalf2 = sb("mhalf2", [P, 1], F32)
        eps2 = sb("eps2", [P, 1], F32)
        carrier2 = sb("carrier2", [P, 1], F32)

        gbank, ubank, tbank, zbank = [psum(n, [P, BANK], F32) for n in ("gbank", "ubank", "turned", "zbank")]
        dbank = [psum(f"dbank{q}", [P, BANK], F32) for q in range(Q)]
        z_half_bank = [zbank, tbank]

        c_ready = sem("c_ready")
        order_loaded = sem("order_loaded")
        feat_loaded = sem("feat_loaded")
        s_loaded = sem("s_loaded")
        wd_loaded = sem("wd_loaded")
        ln_loaded = [sem(f"ln_loaded{q}") for q in range(RING)]
        res2_loaded = [sem(f"res2_loaded{q}") for q in range(Q)]
        out_stored = [sem(f"out_stored{q}") for q in range(Q)]
        h_bn = sem("h_bn")
        h_mv = sem("h_mv")
        h_eps = sem("h_eps")
        h_rstd = sem("h_rstd")
        h_normed = sem("h_normed")
        h_hi_done = sem("h_hi_done")
        h_ready = sem("h_ready")
        hT_done = sem("hT_done")
        hT_copied = sem("hT_copied")
        z_done = sem("z_done")
        z_hi_done = sem("z_hi_done")
        z_ready = sem("z_ready")
        z_spilled = [sem(f"z_spilled{h}") for h in range(2)]
        z_loaded = [[sem(f"z_loaded{p}{h}") for h in range(2)] for p in range(2)]
        gate_done = sem("gate_done")
        up_done = sem("up_done")
        silu_done = sem("silu_done")
        inter_done = sem("inter_done")
        inter_hi_done = sem("inter_hi_done")
        inter_ready = sem("inter_ready")
        down_done = sem("down_done")
        y_act = sem("y_act")
        y_dve = sem("y_dve")
        o_bn = sem("o_bn")
        o_mv = sem("o_mv")
        o_eps = sem("o_eps")
        o_rstd = sem("o_rstd")
        o_normed = sem("o_normed")
        out_ready = sem("out_ready")

        Z_DMAS = 2 * K
        AHEAD = 6

        block = ctx.enter_context(nc.Block())

        def schedule(engine, quad):
            quad(0, 0, 0, 0, True, True, False, True)
            with engine.Fori(0, GROUPS // 2 - 1) as pair:
                for par in range(2):
                    g = 2 * pair + par
                    for j in range(1, Q):
                        quad(g, par, pair, j, True, True, False, True)
                    quad(g + 1, 1 - par, pair + par, 0, True, True, True, True)
            g, pair = GROUPS - 2, GROUPS // 2 - 1
            for j in range(1, Q):
                quad(g, 0, pair, j, j < 3, j < 2, False, False)
            quad(g + 1, 1, pair, 0, False, False, True, False)
            for j in range(1, Q):
                quad(g + 1, 1, pair, j, False, False, False, False)

        @block.sync
        def _(sp):
            def load_ln(m, slot):
                sp.dma_start(x_ln[:, slot, :], x1_t[m]).then_inc(ln_loaded[slot], 16)

            def load_res(g, q):
                sp.dma_start(x_res[:, q, :], x1_t[g * Q + q]).then_inc(res2_loaded[q], 16)

            def regroup(g, par, loads_before):
                sp.wait_ge(z_ready, (g + 1) * Q)
                for half in range(2):
                    if loads_before is not None:
                        sp.wait_ge(z_loaded[1 - par][half], loads_before * 16)
                    for k in range(K):
                        for part, src in ((0, z_hi), (1, z_lo)):
                            sp.dma_start(z_spill[half, part, k].rearrange("f t n -> t f n"),
                                         src[:, half * K + k, :]).then_inc(z_spilled[half], 16)
                for half in range(2):
                    sp.wait_ge(z_spilled[half], (g + 1) * Z_DMAS * 16)
                    sp.dma_start(z[par][:, half * HALF:(half + 1) * HALF, :],
                                 z_spill[half].rearrange("a k f t n -> (a k f) t n")).then_inc(z_loaded[par][half], 16)

            def quad(g, par, pair, j, evac_z, prep, finish, stream):
                if finish:
                    for q in range(Q):
                        sp.wait_ge(out_ready, (g - 1) * Q + q + 1)
                        sp.dma_start(out_t[(g - 1) * Q + q], x_res[:, q, :]).then_inc(out_stored[q], 16)
                    for q in range(Q):
                        sp.wait_ge(out_stored[q], g * 16)
                        load_res(g, q)
                if stream:
                    m = g * Q + j + AHEAD + 1
                    sp.wait_ge(h_normed, m - RING + 1)
                    load_ln(m, (j + AHEAD + 1) % RING)
                if evac_z and j == 2:
                    regroup(g + 1, 1 - par, pair + 1)

            for m in range(RING):
                load_ln(m, m)
            sp.dma_start(feat[:], features).then_inc(feat_loaded, 16)
            for m in range(RING, AHEAD + 1):
                sp.wait_ge(h_normed, m - RING + 1)
                load_ln(m, m - RING)
            sp.dma_start(s_twice[0:KF], s_dram[0]).then_inc(s_loaded, 16)
            sp.dma_start(s_twice[KF:2 * KF], s_dram[0]).then_inc(s_loaded, 16)
            sp.dma_start(s_low[:], s_dram[1]).then_inc(s_loaded, 16)
            regroup(0, 0, None)
            for q in range(Q):
                load_res(0, q)
            schedule(sp, quad)
            for q in range(Q):
                sp.wait_ge(out_ready, (GROUPS - 1) * Q + q + 1)
                sp.dma_start(out_t[(GROUPS - 1) * Q + q], x_res[:, q, :]).then_inc(out_stored[q], 16)
            for q in range(Q):
                sp.wait_ge(out_stored[q], GROUPS * 16)

        @block.gpsimd
        def _(pool):
            pool.dma_start(order[:], perm).then_inc(order_loaded, 16)
            pool.memset(mhalf2[:], -0.5).then_inc(c_ready, 1)
            pool.memset(eps2[:], EPS).then_inc(c_ready, 1)
            pool.memset(id32[:], 0.0).then_inc(c_ready, 1)
            pool.wait_ge(c_ready, 3)
            pool.affine_select(out=id32[:], in_=id32[:], compare_op=ALU.not_equal, fill=1.0,
                               base=0, pattern=[[-1, P]], channel_multiplier=1).then_inc(c_ready, 1)
            pool.wait_ge(c_ready, 4)
            pool.tensor_copy(id16[:], id32[:]).then_inc(c_ready, 1)

            def h_scale(m):
                n = held(pool, m + 1)
                pool.wait_ge(h_mv, n)
                pool.tensor_tensor(hr[:, 0:1], hmv[:, 1:2], eps2[:], ALU.add).then_inc(h_eps, 1)
                pool.wait_ge(h_eps, n)
                pool.tensor_tensor(hr[:, 1:2], hr[:, 0:1], mhalf2[:], ALU.pow).then_inc(h_rstd, 1)

            def o_scale(g, q):
                n = held(pool, g * Q + q + 1)
                pool.wait_ge(o_mv, n)
                pool.tensor_tensor(orr[:, q, 0:1], omv[:, q, 1:2], eps2[:], ALU.add).then_inc(o_eps, 1)
                pool.wait_ge(o_eps, n)
                pool.tensor_tensor(orr[:, q, 1:2], orr[:, q, 0:1], mhalf2[:], ALU.pow).then_inc(o_rstd, 1)

            def quad(g, par, pair, j, evac_z, prep, finish, stream):
                if finish:
                    o_scale(g - 1, 0)
                if prep:
                    h_scale(g * Q + j + AHEAD)
                if finish:
                    for q in range(1, Q):
                        o_scale(g - 1, q)

            for m in range(AHEAD):
                h_scale(m)
            pool.wait_ge(order_loaded, 16)
            for t in range(I):
                pool.indirect_dma_start(wd[:, t, :], None, d_dram.rearrange("t p a e -> (t p) (a e)"),
                                        bass.IndirectOffsetOnAxis(ap=order[:, t:t + 1], axis=0)
                                        ).then_inc(wd_loaded, 16)
            schedule(pool, quad)
            for q in range(Q):
                o_scale(GROUPS - 1, q)

        @block.scalar
        def _(act):
            def h_high(m):
                act.wait_ge(h_normed, m + 1)
                if not (isinstance(m, int) and m == 0):
                    act.wait_ge(hT_done, m)
                act.activation(h_hi[:], hn[:], ACT.Copy, scale=XN_SCALE).then_inc(h_hi_done, 1)

            def z_high(m, q, groups_before):
                if q == 0 and not (isinstance(groups_before, int) and groups_before == 0):
                    for half in range(2):
                        act.wait_ge(z_spilled[half], groups_before * Z_DMAS * 16)
                for half in range(2):
                    act.wait_ge(z_done, m * 2 + half + 1)
                    act.activation(z_hi[:, half * K:(half + 1) * K, q * P:(q + 1) * P],
                                   z_half_bank[half][:].rearrange("p (k n) -> p k n", n=P), ACT.Copy,
                                   scale=Z_SCALE / (XN_SCALE * FEATURE_SCALE)).then_inc(z_hi_done, 1)

            def high(n, slot):
                act.wait_ge(inter_done, n + 1)
                if not (isinstance(n, int) and n < 4):
                    act.wait_ge(down_done, n * Q - 3 * Q)
                act.copy(inter_hi[:, slot, :], inter[:, slot % 2, :]).then_inc(inter_hi_done, 1)

            def silu_at(n, slot):
                act.wait_ge(gate_done, n + 1)
                act.activation(gated[:, slot % 2, :], gbank[:], ACT.Silu, scale=c_gate[:]).then_inc(silu_done, 1)

            def quad(g, par, pair, j, evac_z, prep, finish, stream):
                for s in range(4):
                    i = 4 * j + s
                    n = g * I + i
                    last = isinstance(n, int) and n >= STEPS - 2
                    if not (last and n == STEPS - 1):
                        if isinstance(n, int) and n == 0:
                            high(1, 1)
                        else:
                            high(n + 1, (s + 1) % 4)
                    if not last:
                        silu_at(n + 2, (s + 2) % 4)
                    if s == 0 and evac_z:
                        z_high(g * Q + j + AHEAD - 1, (j + 1) % Q, g + 2)
                    if s == 1 and prep:
                        h_high(g * Q + j + AHEAD)
                    if i == I - 1:
                        for q in (0, 2):
                            act.wait_ge(down_done, n * Q + q + 1)
                            act.activation(y[:, q, :], dbank[q][:], ACT.Copy, scale=c_out[:]).then_inc(y_act, 1)

            for m in range(4):
                h_high(m)
                if m:
                    z_high(m - 1, m - 1, 0)
            z_high(3, 3, 0)
            h_high(4)
            z_high(4, 0, 1)
            h_high(5)
            silu_at(0, 0)
            high(0, 0)
            silu_at(1, 1)
            schedule(act, quad)

        @block.vector
        def _(dve):
            def h_stats(m, slot, count):
                n = held(dve, m + 1)
                dve.wait_ge(ln_loaded[slot], count * 16)
                dve.bn_stats(hstats[:], x_ln[:, slot, :]).then_inc(h_bn, 1)
                dve.wait_ge(h_bn, n)
                dve.memset(carrier2[:], 0.0)
                dve.bn_aggr(hmv[:], hstats[:]).then_inc(h_mv, 1)

            def h_norm(m, slot):
                dve.wait_ge(h_rstd, m + 1)
                dve.tensor_scalar(hn[:], x_ln[:, slot, :], hmv[:, 0:1], hr[:, 1:2],
                                  ALU.subtract, ALU.mult).then_inc(h_normed, 1)

            def h_low(m):
                dve.wait_ge(h_hi_done, m + 1)
                dve.scalar_tensor_tensor(out=h_lo[:], in0=hn[:], scalar=XN_SCALE, in1=h_hi[:],
                                         op0=ALU.mult, op1=ALU.subtract).then_inc(h_ready, 1)

            def hT_copy(m):
                dve.wait_ge(hT_done, m + 1)
                dve.tensor_copy(hT[:].rearrange("p a k n -> p (a k n)"), tbank[:].bitcast(F16)).then_inc(hT_copied, 1)

            def z_low(m, q):
                for half in range(2):
                    dve.wait_ge(z_hi_done, m * 2 + half + 1)
                    lo = dve.scalar_tensor_tensor(out=z_lo[:, half * K:(half + 1) * K, q * P:(q + 1) * P],
                                                  in0=z_half_bank[half][:].rearrange("p (k n) -> p k n", n=P),
                                                  scalar=Z_SCALE / (XN_SCALE * FEATURE_SCALE),
                                                  in1=z_hi[:, half * K:(half + 1) * K, q * P:(q + 1) * P],
                                                  op0=ALU.mult, op1=ALU.subtract)
                lo.then_inc(z_ready, 1)

            def product(n, slot):
                dve.wait_ge(silu_done, n + 1)
                dve.wait_ge(up_done, n + 1)
                dve.scalar_tensor_tensor(out=inter[:, slot % 2, :], in0=ubank[:], scalar=c_up[:],
                                         in1=gated[:, slot % 2, :], op0=ALU.mult, op1=ALU.mult).then_inc(inter_done, 1)

            def low(n, slot):
                dve.wait_ge(inter_hi_done, n + 1)
                dve.tensor_tensor(inter_lo[:, slot, :], inter[:, slot % 2, :], inter_hi[:, slot, :],
                                  ALU.subtract).then_inc(inter_ready, 1)

            def o_stats(g, q):
                n = held(dve, g * Q + q + 1)
                if q % 2 == 0:
                    dve.wait_ge(y_act, g * 2 + q // 2 + 1)
                else:
                    dve.wait_ge(y_dve, g * 2 + q // 2 + 1)
                dve.bn_stats(ostats[:, q % 2, :], y[:, q, :]).then_inc(o_bn, 1)
                dve.wait_ge(o_bn, n)
                dve.memset(carrier2[:], 0.0)
                dve.bn_aggr(omv[:, q, :], ostats[:, q % 2, :]).then_inc(o_mv, 1)

            def o_finish(g, q):
                n = g * Q + q + 1
                dve.wait_ge(o_rstd, n)
                dve.tensor_scalar(y[:, q, :], y[:, q, :], omv[:, q, 0:1], orr[:, q, 1:2],
                                  ALU.subtract, ALU.mult).then_inc(o_normed, 1)
                dve.wait_ge(o_normed, n)
                dve.wait_ge(res2_loaded[q], (g + 1) * 16)
                dve.tensor_tensor(x_res[:, q, :], y[:, q, :], x_res[:, q, :], ALU.add).then_inc(out_ready, 1)

            def quad(g, par, pair, j, evac_z, prep, finish, stream):
                m, slot = g * Q + j + AHEAD, (j + AHEAD) % RING
                count = g + 1 + (j + AHEAD) // RING
                for s in range(4):
                    i = 4 * j + s
                    n = g * I + i
                    if s == 3 and prep:
                        hT_copy(m)
                    if not (isinstance(n, int) and n == STEPS - 1):
                        low(n + 1, (s + 1) % 4)
                    if not (isinstance(n, int) and n >= STEPS - 2):
                        product(n + 2, (s + 2) % 4)
                    if s == 0 and evac_z:
                        z_low(m - 1, (j + 1) % Q)
                    if finish:
                        o_stats(g - 1, s)
                        if s:
                            o_finish(g - 1, s - 1)
                        if s == 3:
                            o_finish(g - 1, 3)
                    if s == 0 and prep:
                        h_stats(m, slot, count)
                    if s == 1 and prep:
                        h_norm(m, slot)
                        h_low(m)
                    if i == I - 1:
                        for q in (1, 3):
                            dve.wait_ge(down_done, n * Q + q + 1)
                            dve.tensor_scalar(y[:, q, :], dbank[q][:], c_out[:], None, ALU.mult).then_inc(y_dve, 1)

            dve.wait_ge(feat_loaded, 16)
            h_stats(0, 0, 1)
            h_norm(0, 0)
            h_low(0)
            for m in range(1, AHEAD):
                h_stats(m, m % RING, m // RING + 1)
                hT_copy(m - 1)
                h_norm(m, m % RING)
                if m >= 4:
                    z_low(m - 1, (m - 1) % Q)
                h_low(m)
                if m < 4:
                    z_low(m - 1, m - 1)
            hT_copy(AHEAD - 1)
            product(0, 0)
            low(0, 0)
            product(1, 1)
            schedule(dve, quad)
            for q in range(Q):
                o_stats(GROUPS - 1, q)
                if q:
                    o_finish(GROUPS - 1, q - 1)
            o_finish(GROUPS - 1, Q - 1)

        @block.tensor
        def _(pe):
            pe.wait_ge(c_ready, 5)
            pe.wait_ge(feat_loaded, 16)

            def turn(m):
                pe.wait_ge(h_ready, m + 1)
                if not (isinstance(m, int) and m == 0):
                    pe.wait_ge(z_ready, m)
                view = tbank[:].bitcast(F16)
                for part, src in ((0, h_hi), (1, h_lo)):
                    for k in range(K):
                        mm = pe.transpose(view[:, (part * K + k) * P:(part * K + k + 1) * P],
                                          src[:, k * P:(k + 1) * P], id16[:])
                mm.then_inc(hT_done, 1)

            def features_of(m):
                pe.wait_ge(hT_copied, m + 1)
                for half in range(2):
                    cols = slice(half * ZCOLS, (half + 1) * ZCOLS)
                    for k in range(K):
                        bank = z_half_bank[half][:, k * P:(k + 1) * P]
                        pe.matmul(bank, feat[:, 0, k, cols], hT[:, 0, k, :], start=True, stop=False)
                        pe.matmul(bank, feat[:, 0, k, cols], hT[:, 1, k, :], start=False, stop=False)
                        mm = pe.matmul(bank, feat[:, 1, k, cols], hT[:, 0, k, :], start=False, stop=True)
                    mm.then_inc(z_done, 1)

            def gate_up(n, i, par, count):
                if i % HALF == 0:
                    pe.wait_ge(z_loaded[par][i // HALF], count * 16)
                cols = slice(i * P, (i + 1) * P)
                for w, bank, free, done in ((GATE, gbank, silu_done, gate_done), (UP, ubank, inter_done, up_done)):
                    if not (isinstance(n, int) and n == 0):
                        pe.wait_ge(free, n)
                    pe.matmul(bank[:], s_twice[:, w, cols], z[par][:, i, :], start=True, stop=False)
                    pe.matmul(bank[:], s_low[:, w, cols], z[par][0:KF, i, :], start=False, stop=True).then_inc(done, 1)

            def down(g, n, i):
                pe.wait_ge(inter_ready, n + 1)
                s = i % 4
                for q in range(Q):
                    if i == 0 and not (isinstance(g, int) and g == 0):
                        pe.wait_ge((y_act, y_dve)[q % 2], g * 2 - 1 + q // 2)
                    c = slice(q * P, (q + 1) * P)
                    start, stop = i == 0, i == I - 1
                    pe.matmul(dbank[q][:], inter_hi[:, s, c], wd[:, i, 0:E], start=start, stop=False)
                    pe.matmul(dbank[q][:], inter_hi[:, s, c], wd[:, i, E:2 * E], start=False, stop=False)
                    pe.matmul(dbank[q][:], inter_lo[:, s, c], wd[:, i, 0:E], start=False, stop=stop
                              ).then_inc(down_done, 1)

            def quad(g, par, pair, j, evac_z, prep, finish, stream):
                m = g * Q + j + AHEAD
                for s in range(4):
                    i = 4 * j + s
                    n = g * I + i
                    if i + 2 < I:
                        gate_up(n + 2, i + 2, par, pair + 1)
                    elif not (isinstance(n, int) and n >= STEPS - 2):
                        gate_up(n + 2, i + 2 - I, 1 - par, pair + 1 + par)
                    down(g, n, i)
                    if s == 2 and prep:
                        turn(m)
                    if s == 3 and prep:
                        features_of(m)

            for m in range(AHEAD):
                turn(m)
                features_of(m)
            pe.wait_ge(s_loaded, 3 * 16)
            gate_up(0, 0, 0, 1)
            gate_up(1, 1, 0, 1)
            pe.wait_ge(wd_loaded, I * 16)
            schedule(pe, quad)


def piece_grid(n_ctrl, n_samples, r):
    import numpy as np
    step = (n_ctrl - 1.0) / (n_samples - 1)
    seg = np.minimum(np.floor(step * P * r).astype(np.int64), n_ctrl - 2)
    n = P * r[None, :] + np.arange(P)[:, None]
    later = np.minimum(np.floor(step * n).astype(np.int64), n_ctrl - 2) - seg
    assert ((later == 0) | (later == 1)).all()
    return step, seg, later


def piece_powers(step, r, seg, later):
    import numpy as np
    catmull = 0.5 * np.array([[0, 2, 0, 0], [-1, 0, 1, 0], [2, -5, 4, -1], [-1, 3, -3, 1]], np.float64)
    binom = np.array([[1, 0, 0, 0], [1, 1, 0, 0], [1, 2, 1, 0], [1, 3, 3, 1]], np.float64)
    half = P // 2
    mid = step * (P * r + half) - seg - later
    return np.stack([np.stack([sum(catmull[j, q] * binom[j, m] * mid ** (j - m) for j in range(m, 4))
                               * (step * half) ** m for q in range(4)]) for m in range(4)])


def fold(a, parts):
    import numpy as np
    return np.concatenate(np.split(a, parts, axis=-1), axis=0)


def row_tables(r, n_ctrl, n_samples):
    import numpy as np
    step, seg, later = piece_grid(n_ctrl, n_samples, r)
    points = np.empty((32, r.size), np.int64)
    coef = np.empty((32, r.size), np.float64)
    for nxt in range(2):
        powers = piece_powers(step, r, seg, nxt)
        for m in range(4):
            for q in range(4):
                row = 16 * nxt + 4 * m + q
                points[row] = np.clip(seg + nxt + q - 1, 0, n_ctrl - 1)
                coef[row] = powers[m, q]
    return fold(points, 4), fold(coef, 4).astype(np.float32), fold(later.astype(np.uint8), 1)


def vandermonde():
    import numpy as np
    v = (np.arange(P) - P // 2) / (P // 2)
    table = np.zeros((P, 2, P), np.float32)
    for g in range(4):
        for nxt in range(2):
            for m in range(4):
                for q in range(4):
                    table[32 * g + 16 * nxt + 4 * m + q, nxt] = v ** m
    return table


def phase_order(n_ctrl, n_samples, K):
    import numpy as np
    step = (n_ctrl - 1.0) / (n_samples - 1)
    units = n_samples // (K * P)
    return np.argsort(-np.mod(step * K * P * np.arange(units), 1), kind="stable")


def feature_tables(order, K, n_ctrl, n_samples):
    import numpy as np
    T = order.size // P
    v = (np.arange(P) - P // 2) / (P // 2)
    feat = np.zeros((P, K, T, FEATURES), np.float64)
    coef = np.zeros((K, FEATURES, 5, order.size), np.float64)
    points = np.zeros((K, FEATURES, 5, order.size), np.int64)
    for k in range(K):
        r = K * order + k
        step, seg, later = piece_grid(n_ctrl, n_samples, r)
        for q in range(5):
            points[k, :, q] = np.clip(seg - 1 + q, 0, n_ctrl - 1)
        powers = [piece_powers(step, r, seg, nxt) for nxt in range(2)]
        for t in range(T):
            cols = slice(t * P, (t + 1) * P)
            kinds, kind, count = np.unique(later[:, cols], axis=0, return_inverse=True, return_counts=True)
            kind = kind.ravel()
            ranges = np.argsort(-count, kind="stable")[:2]
            for a, which in enumerate(ranges):
                inside = kind == which
                for m in range(4):
                    feat[inside, k, t, 4 * a + m] = v[inside] ** m
                    for c in range(P):
                        nxt = kinds[which, c]
                        coef[k, 4 * a + m, nxt:nxt + 4, t * P + c] = powers[nxt][m, :, t * P + c]
            window = np.flatnonzero(~np.isin(kind, ranges))
            assert window.size <= FEATURES - 8
            for w, p in enumerate(window):
                feat[p, k, t, 8 + w] = 1.0
                for c in range(P):
                    nxt = later[p, t * P + c]
                    coef[k, 8 + w, nxt:nxt + 4, t * P + c] = (v[p] ** np.arange(4)) @ powers[nxt][:, :, t * P + c]
    assert np.abs(coef).sum(2).max() < 7.9
    feat *= FEATURE_SCALE
    high = feat.astype(np.float16)
    low = (feat - high).astype(np.float16)
    assert (high.astype(np.float64) + low == feat).all()
    features = np.stack([high, low], 1).reshape(P, 2, K, T * FEATURES)
    return features, points.reshape(K * FEATURES, 5, -1), coef.reshape(K * FEATURES, 5, -1).astype(np.float32)


def build(nc, x, wq, wk, wvT, wo, raw_ctrl, unit_ctrl, unit_coef, row_ctrl, row_coef, later_half, vander,
          features, perm, out):
    tiles, kf = perm.shape[1], unit_coef.shape[0] // 2
    hidden = x.shape[2]
    x1 = nc.dram_tensor("x1", out.shape, F32, kind="Internal").ap()
    s_dram = nc.dram_tensor("unit_features", (2, kf, 2, tiles * P), F16, kind="Internal").ap()
    d_dram = nc.dram_tensor("down_rows", (tiles, P, 2, hidden), F16, kind="Internal").ap()
    z_spill = nc.dram_tensor("token_features", (2, 2, hidden // P, FEATURES, tiles // 2, 512), F16,
                             kind="Internal").ap()
    with ExitStack() as ctx:
        c_gate, c_up, c_out = [ctx.enter_context(nc.sbuf_tensor(name, [P, 1], F32))
                               for name in ("c_gate", "c_up", "c_out")]
        weights_block(nc, raw_ctrl, unit_ctrl, unit_coef, row_ctrl, row_coef, later_half, vander,
                      s_dram, d_dram, c_gate, c_up, c_out)
        attention_block(nc, x, wq, wk, wvT, wo, x1)
        ffn_block(nc, x1, features, perm, s_dram, d_dram, z_spill, c_gate, c_up, c_out, out)


def kernel(**inputs):
    import numpy as np
    import concourse.bacc as bacc
    from concourse.bass_utils import run_bass_kernel_spmd as run

    nc = bacc.Bacc("TRN2", target_bir_lowering=False, num_devices=1)
    arrays = {}

    def dram(name, a):
        arrays[name] = np.ascontiguousarray(a)
        return nc.dram_tensor(name, arrays[name].shape, mybir.dt.from_np(arrays[name].dtype), kind="ExternalInput").ap()

    x = np.asarray(inputs["L0_attn_x"])
    hidden = x.shape[-1]
    cps = [np.asarray(inputs[f"L0_ffn_{n}_cp"]) for n in ("gate", "up", "down")]
    n_ctrl = cps[0].shape[0]
    ffn = 4 * hidden
    K, I = hidden // P, ffn // P
    order = phase_order(n_ctrl, ffn * hidden, K)
    features, unit_points, unit_coef = feature_tables(order, K, n_ctrl, ffn * hidden)
    i, h = np.meshgrid(np.arange(I), np.arange(hidden), indexing="ij")
    row_points, row_coef, later = row_tables((I * h + i).ravel(), n_ctrl, ffn * hidden)
    every = np.minimum(np.arange(-(-n_ctrl // P) * P), n_ctrl - 1).reshape(P, -1)
    args = [
        dram("x", x), dram("wq", inputs["L0_attn_Wq"]), dram("wk", inputs["L0_attn_Wk"]),
        dram("wvT", np.asarray(inputs["L0_attn_Wv"]).T), dram("wo", inputs["L0_attn_Wo"]),
        dram("raw_ctrl", np.stack([c[every] for c in cps], 1)),
        dram("unit_ctrl", np.stack([fold(c[unit_points], 2) for c in cps[:2]])),
        dram("unit_coef", fold(unit_coef, 2)),
        dram("row_ctrl", cps[2][row_points]), dram("row_coef", row_coef), dram("later_half", later.view(np.int32)),
        dram("vander", vandermonde()), dram("features", features),
        dram("perm", order.reshape(I, P).T.astype(np.int32)),
    ]
    out = nc.dram_tensor("out", (x.shape[0] * x.shape[1], hidden), F32, kind="ExternalOutput").ap()
    build(nc, *args, out)
    result = run(nc, [arrays], core_ids=[0])
    return result.results[0]["out"].reshape(x.shape)
```

```python
from contextlib import ExitStack

import concourse.bass as bass
from concourse import mybir

ALU = mybir.AluOpType
ACT = mybir.ActivationFunctionType
AX = mybir.AxisListType
F32 = mybir.dt.float32
F32R = mybir.dt.float32r
F16 = mybir.dt.float16

P = 128
EPS = 1e-5
BANK = 512
WINDOW = 8
FEATURES = 8 + WINDOW
XN_SCALE = 2.0 ** 11
FEATURE_SCALE = 2.0 ** 8
Z_SCALE = 2.0 ** 7
G_SCALE = XN_SCALE ** -2 * 0.25


def f32(ap):
    return ap.bitcast(F32)


def power_of_two(n):
    return 2.0 ** n


def held(engine, value):
    return value if isinstance(value, int) else engine.snap(value)


def attention_block(nc, x, wq, wk, wvT, wo, x1, raw_ctrl, unit_ctrl, unit_coef, row_ctrl, row_coef, later_half,
                    vander, s_dram, d_dram, c_gate, c_up, c_out, features, feats, ffn_in, perm, ident16):
    B, S, E = x.shape
    K = E // P
    NT = S // P
    XR = 4
    CHAIN = 5 * K
    EVACS = 4 * K
    TB = K - 1 + K
    GATE, UP, DOWN = range(3)
    KF = unit_coef.shape[1] // 2
    UCOLS = unit_coef.shape[3]
    TILES = 4 * B
    UNIT_STEPS = 9
    assert d_dram.shape[0] == TILES and unit_coef.shape[0] == 2 * B
    x_t = x.rearrange("b (t p) e -> (b t) p e", p=P)
    x1_t = x1.rearrange("(n p) e -> n p e", p=P)

    with ExitStack() as ctx:
        def sb(name, shape, dt):
            return ctx.enter_context(nc.sbuf_tensor(name, shape, dt))

        def psum(name, shape, dt):
            return ctx.enter_context(nc.psum_tensor(name, shape, dt))

        def sem(name):
            return ctx.enter_context(nc.semaphore(name))

        WK, WQ, WO, WV = range(4)
        shared = sb("shared", [P, 2 * K, E], F32)
        w_stage = [shared[:, n * K:(n + 1) * K] for n in range(2)]
        expd, y_n, x_res = shared[:, 0:2], shared[:, 2:4], shared[:, 4:4 + XR]
        w_hi, w_lo = ffn_in.weights_under(K, E)
        x_in = feats.x_ln
        xn = feats.xn
        xn_hi, xn_lo = feats.z_hi, feats.z_lo
        xT_hi = sb("xT_hi", [P, K, S], F32R)
        xT_lo = sb("xT_lo", [P, K, S], F32R)
        ga_hi = sb("ga_hi", [P, K, E], F32R)
        ga_lo = sb("ga_lo", [P, K, E], F32R)
        m_hi, m_lo = ga_hi, ga_lo
        tu_hi = sb("tu_hi", [P, K, E], F32R)
        tu_lo = sb("tu_lo", [P, K, E], F32R)
        raw = sb("raw", list(raw_ctrl.shape), F32)
        rows_in = sb("rows_in", [P, BANK], F32)
        rcoef = sb("rcoef", [P, BANK], F32)
        half = sb("half", [P, 4, BANK], mybir.dt.uint8)
        vand = sb("vand", [P, 2, P], F32)
        dense = sb("dense", [P, 2, BANK], F32)
        split = sb("split", [P, 2, 2, BANK], F16)
        units = sb("units", [P, 2, 5, UCOLS], F32)
        ucoef = sb("ucoef", [P, 5, UCOLS], F32)
        s_out = sb("s_out", [P, 2, 2, UCOLS], F16)
        cmax = sb("cmax", [P, 3], F32)
        call = sb("call", [P, 3], F32)
        expo = sb("expo", [P, 3], F32)
        rexpo = sb("rexpo", [P, 3], F32)
        wscale = sb("wscale", [P, 3], F32)
        c_gu = sb("c_gu", [P, 1], F32)
        ident32 = sb("ident32", [P, P], F32)
        stats = sb("stats", [P, 2, 6], F32)
        mv = sb("mv", [P, NT, 2], F32)
        rstd = sb("rstd", [P, NT, 2], F32)
        ystats = sb("ystats", [P, 2, 6], F32)
        ymv = sb("ymv", [P, NT, 2], F32)
        yr = sb("yr", [P, NT, 3], F32)
        smax = sb("smax", [P, K], F32)
        ssum = sb("ssum", [P, K], F32)
        srec = sb("srec", [P, K], F32)
        mhalf = sb("mhalf", [P, 1], F32)
        eps = sb("eps", [P, 1], F32)
        carrier = sb("carrier", [P, 1], F32)
        merge_carrier = sb("merge_carrier", [P, 2], F32)

        chain = psum("chain", [P, K, BANK], F32)
        ybank = psum("ybank", [P, 2, BANK], F32)
        tbank = psum("tbank", [P, 2, BANK], F32)

        s_ident = sem("s_ident")
        w_loaded = [sem(f"w_loaded{i}") for i in range(2)]
        w_hi_done = sem("w_hi_done")
        w_lo_done = sem("w_lo_done")
        wov_hi_done = sem("wov_hi_done")
        wov_done = sem("wov_done")
        raw_loaded = sem("raw_loaded")
        vand_loaded = sem("vand_loaded")
        rows_loaded = sem("rows_loaded")
        half_loaded = sem("half_loaded")
        units_loaded = sem("units_loaded")
        max_part = sem("max_part")
        max_all = sem("max_all")
        scale_step = sem("scale_step")
        rows_ready = sem("rows_ready")
        unit_step = sem("unit_step")
        s_ready = sem("s_ready")
        s_stored = sem("s_stored")
        pieces_done = sem("pieces_done")
        first_copied = sem("first_copied")
        merged = sem("merged")
        d_hi_done = sem("d_hi_done")
        d_ready = sem("d_ready")
        d_stored = [sem(f"d_stored{i}") for i in range(2)]
        x_loaded = [sem(f"x_loaded{i}") for i in range(XR)]
        res_loaded = [sem(f"res_loaded{i}") for i in range(XR)]
        x1_stored = [sem(f"x1_stored{i}") for i in range(XR)]
        ln_bn = sem("ln_bn")
        ln_mv = sem("ln_mv")
        ln_rstd = sem("ln_rstd")
        ln_eps = sem("ln_eps")
        xn_normed = sem("xn_normed")
        xn_hi_done = sem("xn_hi_done")
        xn_ready = sem("xn_ready")
        chain_done = sem("chain_done")
        hi_done = sem("hi_done")
        lo_done = sem("lo_done")
        tb_done = sem("tb_done")
        tb_hi = sem("tb_hi")
        tb_lo = sem("tb_lo")
        max_done = sem("max_done")
        exp_done = sem("exp_done")
        rec_done = sem("rec_done")
        a_hi_done = sem("a_hi_done")
        a_done = sem("a_done")
        y_done = sem("y_done")
        y_bn = sem("y_bn")
        y_mv = sem("y_mv")
        y_eps = sem("y_eps")
        y_rstd = sem("y_rstd")
        y_mr = sem("y_mr")
        y_free = sem("y_free")
        y_normed = sem("y_normed")
        x1_ready = sem("x1_ready")

        z_banks = [ybank[:, 1, :], ybank[:, 0, :]]
        last_banks = [chain[:, 3, :], chain[:, 2, :]]
        SPILLS = 4 * K
        assert XR == 4 and NT == 2 * K

        def unit_banks(u):
            return (ybank, ybank, tbank, chain)[u]

        block = ctx.enter_context(nc.Block())

        @block.sync
        def _(sp):
            def load_x(b, t):
                if not (isinstance(b, int) and b == 0 and t < XR):
                    sp.wait_ge(xn_normed, b * NT + t + 1 - XR)
                sp.dma_start(x_in[:, t % XR, :], x_t[b * NT + t]).then_inc(x_loaded[t % XR], 16)

            def load_res(b, t):
                if not (isinstance(b, int) and b == 0 and t < XR):
                    sp.wait_ge(x1_stored[t % XR], (b * (NT // XR) + t // XR) * 16)
                sp.dma_start(x_res[:, t % XR, :], x_t[b * NT + t]).then_inc(res_loaded[t % XR], 16)

            def load_w(n, w):
                if n >= 2:
                    sp.wait_ge(w_lo_done, n - 1)
                sp.dma_start(w_stage[n % 2], w.rearrange("(k p) e -> p k e", p=P)).then_inc(w_loaded[n % 2], 16)

            def load_rows(b):
                sp.dma_start(rows_in[:], row_ctrl[b]).then_inc(rows_loaded, 16)
                sp.dma_start(rcoef[:], row_coef[b]).then_inc(rows_loaded, 16)

            def load_half(b):
                sp.dma_start(half[:], later_half[b].bitcast(mybir.dt.uint8).rearrange("p (u n) -> p u n", u=4)
                             ).then_inc(half_loaded, 16)

            def load_units(c):
                sp.dma_start(units[:], unit_ctrl[c].rearrange("p (w q n) -> p w q n", w=2, q=5)
                             ).then_inc(units_loaded, 16)
                sp.dma_start(ucoef[:], unit_coef[c]).then_inc(units_loaded, 16)

            def store_rows(b, u):
                ready, tile = held(sp, b * 4 + u + 1), held(sp, b + B * u)
                sp.wait_ge(d_ready, ready)
                sp.dma_start(d_dram[tile], split[:, u % 2]).then_inc(d_stored[u % 2], 16)

            def store_units(c, more):
                c, ready = held(sp, c), held(sp, c + 1)
                sp.wait_ge(s_ready, ready)
                if more:
                    load_units(ready)
                for side in range(2):
                    for part in range(2):
                        sp.dma_start(s_dram[part, side, :, c], s_out[side * KF:(side + 1) * KF, :, part]
                                     ).then_inc(s_stored, 16)

            def body(b, more):
                if more:
                    for t in range(XR):
                        load_x(b + 1, t)
                else:
                    sp.wait_ge(xn_normed, B * NT)
                    for m in range(XR):
                        feats.load(sp, x1_t, m, m)
                store_units(2 * b, True)
                store_rows(b, 0)
                store_units(2 * b + 1, more)
                store_rows(b, 1)
                if more:
                    for t in range(XR, NT):
                        load_x(b + 1, t)
                else:
                    sp.wait_ge(s_stored, (2 * B + 1) * 64)
                    sp.wait_ge(chain_done, b * CHAIN + 2 * K)
                    ffn_in.load_units(sp, s_dram, KF)
                    feats.spill(sp, 0, SPILLS // 2, 0)
                for t in range(NT):
                    sp.wait_ge(x1_ready, b * NT + t + 1)
                    sp.dma_start(x1_t[b * NT + t], x_res[:, t % XR, :]).then_inc(x1_stored[t % XR], 16)
                    if 1 <= t <= NT - XR:
                        load_res(b, t - 1 + XR)
                    elif more and t > NT - XR:
                        load_res(b + 1, t - 1 + XR - NT)
                    if t == 0 and more:
                        used, after = held(sp, b * 4 + 4), held(sp, b + 1)
                        sp.wait_ge(pieces_done, used)
                        load_rows(after)
                    if t == 2:
                        store_rows(b, 2)
                    if t == 6:
                        store_rows(b, 3)
                    if not more and t < 3:
                        sp.wait_ge(feats.h_normed, t + 1)
                        feats.load(sp, x1_t, XR + t, t)
                    if not more and t < 2:
                        feats.spill(sp, (t + 2) * SPILLS // 4, (t + 3) * SPILLS // 4, 0)
                    if not more and t == 3:
                        sp.wait_ge(chain_done, b * CHAIN + 3 * K)
                        ffn_in.load_z(sp, feats, 0, 0)
                if more:
                    load_res(b + 1, XR - 1)
                if more:
                    stored, after = held(sp, (b + 1) * 32), held(sp, b + 1)
                    for slot in range(2):
                        sp.wait_ge(d_stored[slot], stored)
                    load_half(after)

            for t in range(XR):
                load_x(0, t)
            load_x(0, XR)
            load_x(0, XR + 1)
            load_w(0, wk)
            load_x(0, XR + 2)
            load_w(1, wq)
            load_x(0, XR + 3)
            sp.dma_start(raw[:], raw_ctrl).then_inc(raw_loaded, 16)
            sp.dma_start(vand[:], vander).then_inc(vand_loaded, 16)
            load_rows(0)
            load_half(0)
            load_units(0)
            sp.dma_start(ffn_in.order[:], perm).then_inc(ffn_in.order_loaded, 16)
            sp.dma_start(feats.feat[:], features).then_inc(feats.feat_loaded, 16)
            load_w(2, wo)
            load_w(3, wvT)
            sp.wait_ge(wov_done, 2)
            for t in range(XR):
                load_res(0, t)
            with sp.Fori(0, B - 1) as b:
                body(b, True)
            body(B - 1, False)
            for q in range(XR):
                sp.wait_ge(x1_stored[q], B * (NT // XR) * 16)
            for slot in range(2):
                sp.wait_ge(d_stored[slot], B * 32)

        @block.gpsimd
        def _(pool):
            pool.sem_inc(s_stored, 64)
            feats.constants(pool)
            pool.memset(mhalf[:], -0.5).then_inc(s_ident, 1)
            pool.memset(eps[:], EPS).then_inc(s_ident, 1)
            pool.memset(ident32[:], 0.0).then_inc(s_ident, 1)
            pool.wait_ge(s_ident, 3)
            pool.affine_select(out=ident32[:], in_=ident32[:], compare_op=ALU.not_equal, fill=1.0,
                               base=0, pattern=[[-1, P]], channel_multiplier=1).then_inc(s_ident, 1)
            pool.wait_ge(s_ident, 4)
            pool.tensor_copy(ident16[:], ident32[:]).then_inc(s_ident, 1)

            def ln_scale(b, t):
                n = held(pool, b * NT + t + 1)
                pool.wait_ge(ln_mv, n)
                pool.tensor_tensor(rstd[:, t, 0:1], mv[:, t, 1:2], eps[:], ALU.add).then_inc(ln_eps, 1)
                pool.wait_ge(ln_eps, n)
                pool.tensor_tensor(rstd[:, t, 1:2], rstd[:, t, 0:1], mhalf[:], ALU.pow).then_inc(ln_rstd, 1)

            def y_scale(b, t):
                n = held(pool, b * NT + t + 1)
                pool.wait_ge(y_mv, n)
                pool.tensor_tensor(yr[:, t, 0:1], ymv[:, t, 1:2], eps[:], ALU.add).then_inc(y_eps, 1)
                pool.wait_ge(y_eps, n)
                pool.tensor_tensor(yr[:, t, 1:2], yr[:, t, 0:1], mhalf[:], ALU.pow).then_inc(y_rstd, 1)
                pool.wait_ge(y_rstd, n)
                pool.tensor_tensor(yr[:, t, 2:3], ymv[:, t, 0:1], yr[:, t, 1:2], ALU.mult).then_inc(y_mr, 1)

            def unit_weights(c):
                stored, summed = held(pool, (c + 1) * 64), held(pool, c * UNIT_STEPS + 5)
                pool.wait_ge(units_loaded, (c + 1) * 32)
                for w in range(2):
                    pool.tensor_tensor(units[:, w], units[:, w], ucoef[:], ALU.mult).then_inc(unit_step, 1)
                pool.wait_ge(unit_step, c * UNIT_STEPS + 2)
                pool.tensor_tensor(units[:, :, 0:2], units[:, :, 0:2], units[:, :, 2:4], ALU.add).then_inc(unit_step, 1)
                pool.wait_ge(unit_step, c * UNIT_STEPS + 3)
                pool.tensor_tensor(units[:, :, 0], units[:, :, 0], units[:, :, 1], ALU.add).then_inc(unit_step, 1)
                pool.wait_ge(unit_step, c * UNIT_STEPS + 4)
                pool.tensor_tensor(units[:, :, 0], units[:, :, 0], units[:, :, 4], ALU.add).then_inc(unit_step, 1)
                pool.wait_ge(s_stored, stored)
                pool.wait_ge(unit_step, summed)
                for w in range(2):
                    pool.tensor_tensor(units[:, w, 1], units[:, w, 0], wscale[:, w:w + 1].to_broadcast([P, UCOLS]),
                                       ALU.mult).then_inc(unit_step, 1)
                    pool.tensor_tensor(s_out[:, w, 0], units[:, w, 0], wscale[:, w:w + 1].to_broadcast([P, UCOLS]),
                                       ALU.mult).then_inc(unit_step, 1)
                pool.wait_ge(unit_step, c * UNIT_STEPS + UNIT_STEPS)
                pool.tensor_tensor(s_out[:, :, 1], units[:, :, 1], s_out[:, :, 0], ALU.subtract).then_inc(s_ready, 1)

            def body(b, more):
                for c in range(2):
                    unit_weights(2 * b + c)
                if more:
                    for t in range(NT):
                        ln_scale(b + 1, t)
                else:
                    for m in range(XR):
                        feats.scale(pool, m)
                for t in range(NT):
                    y_scale(b, t)
                    if not more and t == 3:
                        feats.scale(pool, XR)

            for t in range(NT):
                ln_scale(0, t)
            pool.wait_ge(max_part, 1)
            pool.partition_all_reduce(call[:], cmax[:], P, bass.bass_isa.ReduceOp.max).then_inc(max_all, 1)
            for n in range(2):
                pool.wait_ge(w_loaded[n], 32)
                pool.tensor_copy(w_hi[WO + n], w_stage[n]).then_inc(wov_hi_done, 1)
                pool.wait_ge(wov_hi_done, n + 1)
                pool.tensor_tensor(w_lo[WO + n], w_stage[n], f32(w_hi[WO + n]), ALU.subtract
                                   ).then_inc(wov_done, 1)
            pool.wait_ge(scale_step, 9)
            with pool.Fori(0, B - 1) as b:
                body(b, True)
            body(B - 1, False)

        @block.scalar
        def _(act):
            def ln_hi(b, t):
                act.wait_ge(xn_normed, b * NT + t + 1)
                if not (isinstance(b, int) and b == 0):
                    act.wait_ge(tb_done, b * TB)
                act.activation(xn_hi[:, t, :], xn[:, t % 2, :], ACT.Copy, scale=XN_SCALE).then_inc(xn_hi_done, 1)

            def evac_hi(b, stage, m, dst, lo, scale):
                act.wait_ge(chain_done, b * CHAIN + stage * K + m + 1)
                act.activation(dst[:, m, lo:E], chain[:, m, 0:E - lo], ACT.Copy, scale=scale).then_inc(hi_done, 1)

            def mirror_hi(b, m):
                act.wait_ge(tb_done, b * TB + m + 1)
                act.copy(ga_hi[:, m + 1:K, m * P:(m + 1) * P],
                         tbank[:, 0, 0:(K - 1 - m) * P].rearrange("p (c n) -> p c n", n=P)).then_inc(tb_hi, 1)

            def first_copy(b, u):
                act.wait_ge(pieces_done, b * 4 + u + 1)
                if u >= 2:
                    act.wait_ge(d_ready, b * 4 + u - 1)
                act.copy(dense[:, u % 2, :], unit_banks(u)[:, 0, :]).then_inc(first_copied, 1)

            def d_hi(b, u):
                act.wait_ge(merged, b * 4 + u + 1)
                if u >= 2:
                    act.wait_ge(d_stored[u % 2], b * 32 + 16)
                act.copy(split[:, u % 2, 0], dense[:, u % 2, :]).then_inc(d_hi_done, 1)

            def body(b, more):
                for m in range(K):
                    evac_hi(b, 0, m, ga_hi, m * P, G_SCALE)
                    if m:
                        mirror_hi(b, m - 1)
                for m in range(K):
                    evac_hi(b, 1, m, tu_hi, 0, 1.0)
                    act.wait_ge(tb_done, b * TB + K + m)
                    act.copy(xT_hi[:, m, :], tbank[:, 0, :].bitcast(F16)).then_inc(tb_hi, 1)
                    if m == 1:
                        first_copy(b, 0)
                    if m == 2:
                        d_hi(b, 0)
                first_copy(b, 1)
                d_hi(b, 1)
                act.wait_ge(wov_done, 2)
                if not more:
                    feats.high(act, 0)
                for m in range(K):
                    act.wait_ge(max_done, b * K + m + 1)
                    if m >= 2:
                        act.wait_ge(a_done, b * K + m - 1)
                    act.activation(expd[:, m % 2, :], chain[:, m, :], ACT.Exp, bias=smax[:, m:m + 1],
                                   accum_out=ssum[:, m:m + 1]).then_inc(exp_done, 1)
                for s, dst, scale in ((3, tu_hi, 1.0), (4, m_hi, 1.0 / XN_SCALE)):
                    for m in range(K):
                        evac_hi(b, s, m, dst, 0, scale)
                        t = (s - 3) * K + m - 1
                        if more and t >= 0:
                            ln_hi(b + 1, t)
                        elif not more and m % 2:
                            m4 = t // 2
                            if m4 == 0:
                                act.wait_ge(tb_done, B * TB)
                            feats.z_high(act, m4, m4, 0, z_banks)
                            if m4 < XR - 1:
                                feats.high(act, m4 + 1)
                if more:
                    ln_hi(b + 1, NT - 1)
                for t in range(NT):
                    act.wait_ge(y_rstd, b * NT + t + 1)
                    if t >= 2:
                        act.wait_ge(x1_ready, b * NT + t - 1)
                    act.activation(y_n[:, t % 2, :], ybank[:, t % 2, :], ACT.Copy,
                                   scale=yr[:, t, 1:2]).then_inc(y_normed, 1)
                    if not more and t == 4:
                        feats.high(act, XR)
                    if t in (1, 4):
                        first_copy(b, 2 + t // 4)
                    if t in (2, 5):
                        d_hi(b, 2 + t // 5)
                if not more:
                    feats.z_high(act, XR, 0, 1, last_banks)

            def weight_hi(n):
                act.wait_ge(w_loaded[n], 16)
                act.copy(w_hi[n], w_stage[n]).then_inc(w_hi_done, 1)

            for t in range(NT):
                ln_hi(0, t)
            for n in (WK, WQ):
                weight_hi(n)
            with act.Fori(0, B - 1) as b:
                body(b, True)
            body(B - 1, False)

        @block.vector
        def _(dve):
            def ln_stats(b, t):
                n = held(dve, b * NT + t + 1)
                dve.wait_ge(x_loaded[t % XR], (b * (NT // XR) + t // XR + 1) * 16)
                dve.bn_stats(stats[:, t % 2, :], x_in[:, t % XR, :]).then_inc(ln_bn, 1)
                dve.wait_ge(ln_bn, n)
                dve.memset(carrier[:], 0.0)
                dve.bn_aggr(mv[:, t, :], stats[:, t % 2, :]).then_inc(ln_mv, 1)

            def ln_norm(b, t):
                n = held(dve, b * NT + t + 1)
                dve.wait_ge(ln_rstd, n)
                if not (isinstance(b, int) and b == 0 and t < 2):
                    dve.wait_ge(xn_ready, n - 2)
                dve.tensor_scalar(xn[:, t % 2, :], x_in[:, t % XR, :], mv[:, t, 0:1], rstd[:, t, 1:2],
                                  ALU.subtract, ALU.mult).then_inc(xn_normed, 1)

            def ln_lo(b, t):
                dve.wait_ge(xn_hi_done, b * NT + t + 1)
                dve.scalar_tensor_tensor(out=xn_lo[:, t, :], in0=xn[:, t % 2, :], scalar=XN_SCALE, in1=xn_hi[:, t, :],
                                         op0=ALU.mult, op1=ALU.subtract).then_inc(xn_ready, 1)

            def ln_step(b, j):
                if j < NT:
                    ln_stats(b, j)
                if 1 <= j <= NT:
                    ln_norm(b, j - 1)
                if 2 <= j:
                    ln_lo(b, j - 2)

            def evac_lo(b, n, m, hi, lo_t, lo, scale):
                dve.wait_ge(hi_done, b * EVACS + n * K + m + 1)
                dve.scalar_tensor_tensor(out=lo_t[:, m, lo:E], in0=chain[:, m, 0:E - lo], scalar=scale,
                                         in1=f32(hi[:, m, lo:E]), op0=ALU.mult, op1=ALU.subtract).then_inc(lo_done, 1)

            def mirror_lo(b, m):
                dve.wait_ge(tb_done, b * TB + m + 1)
                dve.tensor_copy(ga_lo[:, m + 1:K, m * P:(m + 1) * P],
                                tbank[:, 1, 0:(K - 1 - m) * P].rearrange("p (c n) -> p c n", n=P)).then_inc(tb_lo, 1)

            def merge(b, u):
                dve.wait_ge(first_copied, b * 4 + u + 1)
                dve.memset(merge_carrier[:, u % 2:u % 2 + 1], 0.0)
                dve.copy_predicated(dense[:, u % 2, :], half[:, u, :], unit_banks(u)[:, 1, :]).then_inc(merged, 1)

            def d_lo(b, u):
                dve.wait_ge(d_hi_done, b * 4 + u + 1)
                dve.tensor_tensor(split[:, u % 2, 1], dense[:, u % 2, :], split[:, u % 2, 0],
                                  ALU.subtract).then_inc(d_ready, 1)

            def body(b, more):
                for m in range(K):
                    evac_lo(b, 0, m, ga_hi, ga_lo, m * P, G_SCALE)
                    if m == 1:
                        dve.wait_ge(rows_loaded, b * 32 + 32)
                        dve.scalar_tensor_tensor(out=rows_in[:], in0=rows_in[:], scalar=wscale[:, DOWN:DOWN + 1],
                                                 in1=rcoef[:], op0=ALU.mult, op1=ALU.mult).then_inc(rows_ready, 1)
                    if m:
                        mirror_lo(b, m - 1)
                for m in range(K):
                    evac_lo(b, 1, m, tu_hi, tu_lo, 0, 1.0)
                    dve.wait_ge(tb_done, b * TB + K + m)
                    dve.tensor_copy(xT_lo[:, m, :], tbank[:, 1, :].bitcast(F16)).then_inc(tb_lo, 1)
                    if m == 1:
                        dve.wait_ge(half_loaded, b * 16 + 16)
                        merge(b, 0)
                    if m == 2:
                        d_lo(b, 0)
                merge(b, 1)
                d_lo(b, 1)
                if more:
                    ln_step(b + 1, 0)
                else:
                    feats.stats(dve, 0, 0, 1)
                    feats.norm(dve, 0, 0)
                    feats.low(dve, 0)
                for m in range(K + 1):
                    if m < K:
                        dve.wait_ge(chain_done, b * CHAIN + 2 * K + m + 1)
                        dve.tensor_reduce(smax[:, m:m + 1], chain[:, m, :], AX.X, ALU.max,
                                          negate=True).then_inc(max_done, 1)
                    if m >= 1:
                        e = expd[:, (m - 1) % 2, :]
                        dve.wait_ge(exp_done, b * K + m)
                        dve.reciprocal(srec[:, m - 1:m], ssum[:, m - 1:m]).then_inc(rec_done, 1)
                        dve.wait_ge(rec_done, b * K + m)
                        dve.tensor_scalar(ga_hi[:, m - 1, :], e, srec[:, m - 1:m], None,
                                          ALU.mult).then_inc(a_hi_done, 1)
                        dve.wait_ge(a_hi_done, b * K + m)
                        dve.scalar_tensor_tensor(out=ga_lo[:, m - 1, :], in0=e, scalar=srec[:, m - 1:m],
                                                 in1=f32(ga_hi[:, m - 1, :]), op0=ALU.mult,
                                                 op1=ALU.subtract).then_inc(a_done, 1)
                for s, hi, lo_t, scale in ((2, tu_hi, tu_lo, 1.0), (3, m_hi, m_lo, 1.0 / XN_SCALE)):
                    for m in range(K):
                        evac_lo(b, s, m, hi, lo_t, 0, scale)
                        j = (s - 2) * K + m
                        if more:
                            ln_step(b + 1, j + 1)
                        elif m % 2 == 0:
                            feats.turn_copy(dve, j // 2, z_banks)
                            if j // 2 < XR - 1:
                                feats.stats(dve, j // 2 + 1, j // 2 + 1, 1)
                        else:
                            if j // 2 < XR - 1:
                                feats.norm(dve, j // 2 + 1, j // 2 + 1)
                            feats.z_low(dve, j // 2, j // 2, z_banks)
                            if j // 2 < XR - 1:
                                feats.low(dve, j // 2 + 1)

                for t in range(NT + 1):
                    if t < NT:
                        n = held(dve, b * NT + t + 1)
                        dve.wait_ge(y_done, n)
                        dve.bn_stats(ystats[:, t % 2, :], ybank[:, t % 2, :]).then_inc(y_bn, 1)
                        dve.wait_ge(y_bn, n)
                        dve.memset(carrier[:], 0.0)
                        dve.bn_aggr(ymv[:, t, :], ystats[:, t % 2, :]).then_inc(y_mv, 1)
                    if t == 0 and more:
                        ln_step(b + 1, NT + 1)
                    if t >= 1:
                        u = t - 1
                        dve.wait_ge(y_normed, b * NT + t)
                        dve.wait_ge(res_loaded[u % XR], (b * (NT // XR) + u // XR + 1) * 16)
                        dve.wait_ge(y_mr, b * NT + t)
                        dve.scalar_tensor_tensor(out=x_res[:, u % XR, :], in0=y_n[:, u % 2, :],
                                                 scalar=yr[:, u, 2:3], in1=x_res[:, u % XR, :],
                                                 op0=ALU.subtract, op1=ALU.add).then_inc(x1_ready, 1)
                    if t in (2, 5):
                        merge(b, 2 + t // 5)
                    if t in (3, 6):
                        d_lo(b, 2 + t // 6)
                    if not more and t == 3:
                        feats.stats(dve, XR, 0, 2)
                    if not more and t == 4:
                        feats.norm(dve, XR, 0)
                        feats.low(dve, XR)
                    if not more and t == 7:
                        feats.turn_copy(dve, XR, last_banks)
                if not more:
                    feats.z_low(dve, XR, 0, last_banks)

            def scales():
                U32 = mybir.dt.uint32
                dve.wait_ge(max_all, 1)
                dve.tensor_scalar(cmax[:], call[:], power_of_two(-60), None, ALU.max).then_inc(scale_step, 1)
                dve.wait_ge(scale_step, 1)
                dve.tensor_scalar(expo[:].bitcast(U32), cmax[:].bitcast(U32), 0x7F800000, None,
                                  ALU.bitwise_and).then_inc(scale_step, 1)
                dve.wait_ge(scale_step, 2)
                dve.reciprocal(rexpo[:], expo[:]).then_inc(scale_step, 1)
                dve.tensor_scalar(c_gate[:], expo[:, GATE:GATE + 1], power_of_two(-12) / Z_SCALE, None,
                                  ALU.mult).then_inc(scale_step, 1)
                dve.tensor_tensor(c_gu[:], expo[:, GATE:GATE + 1], expo[:, UP:UP + 1], ALU.mult).then_inc(scale_step, 1)
                dve.wait_ge(scale_step, 5)
                dve.tensor_scalar(wscale[:, GATE:UP + 1], rexpo[:, GATE:UP + 1], power_of_two(12), None,
                                  ALU.mult).then_inc(scale_step, 1)
                dve.tensor_scalar(wscale[:, DOWN:DOWN + 1], rexpo[:, DOWN:DOWN + 1], power_of_two(13), None,
                                  ALU.mult).then_inc(scale_step, 1)
                dve.tensor_scalar(c_up[:], rexpo[:, GATE:GATE + 1], power_of_two(-17) / Z_SCALE, None,
                                  ALU.mult).then_inc(scale_step, 1)
                dve.tensor_scalar(c_out[:], c_gu[:], expo[:, DOWN:DOWN + 1], power_of_two(-8),
                                  ALU.mult, ALU.mult).then_inc(scale_step, 1)
                dve.wait_ge(scale_step, 9)

            def weight_lo(n):
                dve.wait_ge(w_hi_done, n + 1)
                dve.tensor_tensor(w_lo[n], w_stage[n], f32(w_hi[n]), ALU.subtract).then_inc(w_lo_done, 1)

            for j in range(NT + 2):
                ln_step(0, j)
            dve.wait_ge(raw_loaded, 16)
            dve.tensor_reduce(cmax[:], raw[:], AX.X, ALU.max, apply_absolute_value=True).then_inc(max_part, 1)
            for n in (WK, WQ):
                weight_lo(n)
            scales()
            with dve.Fori(0, B - 1) as b:
                body(b, True)
            body(B - 1, False)

        @block.tensor
        def _(pe):
            def product(out, l_hi, l_lo, r_hi, r_lo, start, stop):
                pe.matmul(out, l_hi, r_hi, start=start, stop=False)
                pe.matmul(out, l_hi, r_lo, start=False, stop=False)
                return pe.matmul(out, l_lo, r_hi, start=False, stop=stop)

            def mirror(b, m):
                pe.wait_ge(lo_done, b * EVACS + m + 1)
                if m:
                    pe.wait_ge(tb_hi, b * TB + m)
                    pe.wait_ge(tb_lo, b * TB + m)
                for part, src in ((0, ga_hi), (1, ga_lo)):
                    for c in range(m + 1, K):
                        mm = pe.transpose(tbank[:, part, (c - m - 1) * P:(c - m) * P],
                                          f32(src[:, m, c * P:(c + 1) * P]), ident32[:])
                mm.then_inc(tb_done, 1)

            def gram(b, m):
                for t in range(NT):
                    if m == 0:
                        pe.wait_ge(xn_ready, b * NT + t + 1)
                    c = slice(m * P, (m + 1) * P)
                    mm = product(chain[:, m, 0:E - m * P], xn_hi[:, t, c], xn_lo[:, t, c],
                                 xn_hi[:, t, m * P:E], xn_lo[:, t, m * P:E], t == 0, t == NT - 1)
                mm.then_inc(chain_done, 1)

            def square(m, hi, lo, r_hi, r_lo, ready):
                for k in range(K):
                    if ready:
                        ready(k)
                    c = slice(m * P, (m + 1) * P)
                    mm = product(chain[:, m, :], hi(k)[:, c], lo(k)[:, c], r_hi(k), r_lo(k), k == 0, k == K - 1)
                mm.then_inc(chain_done, 1)

            def piece(b, u):
                rows = slice(32 * u, 32 * u + 32)
                if u == 0:
                    pe.wait_ge(vand_loaded, 16)
                pe.wait_ge(rows_ready, b + 1)
                if u == 1:
                    pe.wait_ge(merged, b * 4 + 1)
                if u == 2:
                    pe.wait_ge(tb_hi, b * TB + TB)
                    pe.wait_ge(tb_lo, b * TB + TB)
                if u == 3:
                    pe.wait_ge(lo_done, b * EVACS + 3 * K + 2)
                pe.matmul(unit_banks(u)[:, 0, :], vand[rows, 0, :], rows_in[rows, :], start=True, stop=True)
                pe.matmul(unit_banks(u)[:, 1, :], vand[rows, 1, :], rows_in[rows, :], start=True,
                          stop=True).then_inc(pieces_done, 1)

            def tile_of(t):
                return lambda k: t[:, k, :]

            def weight(t, w):
                return lambda k: t[w][:, k, :]

            def token_features(m, tile):
                if m % 2 == 0:
                    feats.turn(pe, tile, z_banks, ident16)
                else:
                    feats.products(pe, tile, z_banks)

            def body(b, more):
                for m in range(K):
                    gram(b, m)
                    if m:
                        mirror(b, m - 1)
                piece(b, 0)
                for m in range(K):
                    if m < K - 1:
                        pe.wait_ge(tb_hi, b * TB + m + 1)
                        pe.wait_ge(tb_lo, b * TB + m + 1)
                    else:
                        pe.wait_ge(lo_done, b * EVACS + K)
                    pe.wait_ge(w_lo_done, WK + 1)
                    square(m, tile_of(ga_hi), tile_of(ga_lo), weight(w_hi, WK), weight(w_lo, WK), None)
                    u = K - 1 + m
                    pe.wait_ge(tb_hi, b * TB + u)
                    pe.wait_ge(tb_lo, b * TB + u)
                    for part, src in ((0, xn_hi), (1, xn_lo)):
                        for t in range(NT):
                            mm = pe.transpose(tbank[:, part, :].bitcast(F16)[:, t * P:(t + 1) * P],
                                              src[:, t, m * P:(m + 1) * P], ident16[:])
                    mm.then_inc(tb_done, 1)
                piece(b, 1)
                pe.wait_ge(w_lo_done, WQ + 1)
                for m in range(K):
                    square(m, weight(w_hi, WQ), weight(w_lo, WQ), tile_of(tu_hi), tile_of(tu_lo),
                           (lambda k: pe.wait_ge(lo_done, b * EVACS + K + k + 1)) if m == 0 else None)
                piece(b, 2)
                pe.wait_ge(wov_done, 1)
                for m in range(K):
                    square(m, tile_of(ga_hi), tile_of(ga_lo), weight(w_hi, WO), weight(w_lo, WO),
                           (lambda k: pe.wait_ge(a_done, b * K + k + 1)) if m == 0 else None)
                    if not more:
                        token_features(m, m // 2)
                pe.wait_ge(wov_done, 2)
                for m in range(K):
                    square(m, weight(w_hi, WV), weight(w_lo, WV), tile_of(tu_hi), tile_of(tu_lo),
                           (lambda k: pe.wait_ge(lo_done, b * EVACS + 2 * K + k + 1)) if m == 0 else None)
                    if not more:
                        token_features(m, K // 2 + m // 2)
                piece(b, 3)
                pe.wait_ge(merged, b * 4 + 2)
                if not more:
                    pe.wait_ge(feats.z_ready, XR)
                for t in range(NT):
                    if t >= 2:
                        pe.wait_ge(y_normed, b * NT + t - 1)
                    c = slice(t * P, (t + 1) * P)
                    for k in range(K):
                        if t == 0:
                            pe.wait_ge(lo_done, b * EVACS + 3 * K + k + 1)
                        mm = product(ybank[:, t % 2, :], xT_hi[:, k, c], xT_lo[:, k, c], m_hi[:, k, :],
                                     m_lo[:, k, :], k == 0, k == K - 1)
                    mm.then_inc(y_done, 1)
                    if not more and t == 5:
                        feats.turn(pe, XR, last_banks, ident16)
                if not more:
                    feats.products(pe, XR, last_banks)
                pe.wait_ge(merged, b * 4 + 4)

            pe.wait_ge(s_ident, 5)
            with pe.Fori(0, B - 1) as b:
                body(b, True)
            pe.wait_ge(feats.feat_loaded, 16)
            body(B - 1, False)


class TokenFeatures:

    def __init__(self, ctx, nc, K, tiles, spilled):
        def sb(name, shape, dt):
            return ctx.enter_context(nc.sbuf_tensor(name, shape, dt))

        def sem(name):
            return ctx.enter_context(nc.semaphore(name))

        E = K * P
        self.K, self.Q, self.spilled = K, 4, spilled
        self.SPILLS = 4 * K
        self.ZCOLS = tiles // 2 * FEATURES
        self.x_ln = sb("x_ln", [P, 4, E], F32)
        self.feat = sb("feat", [P, 2, K, tiles * FEATURES], F16)
        self.xn = sb("xn", [P, 2, E], F32)
        self.h_hi = sb("h_hi", [P, E], F16)
        self.h_lo = sb("h_lo", [P, E], F16)
        self.hT = sb("hT", [P, 2, K, P], F16)
        self.z_hi = sb("z_hi", [P, 2 * K, 4 * P], F16)
        self.z_lo = sb("z_lo", [P, 2 * K, 4 * P], F16)
        self.hstats = sb("hstats", [P, 6], F32)
        self.hmv = sb("hmv", [P, 2], F32)
        self.hr = sb("hr", [P, 2], F32)
        self.hcarrier = sb("hcarrier", [P, 1], F32)
        self.hmhalf = sb("hmhalf", [P, 1], F32)
        self.heps = sb("heps", [P, 1], F32)
        self.feat_loaded = sem("feat_loaded")
        self.const_ready = sem("const_ready")
        self.ln_loaded = [sem(f"ln_loaded{q}") for q in range(4)]
        self.h_bn = sem("h_bn")
        self.h_mv = sem("h_mv")
        self.h_eps = sem("h_eps")
        self.h_rstd = sem("h_rstd")
        self.h_normed = sem("h_normed")
        self.h_hi_done = sem("h_hi_done")
        self.h_ready = sem("h_ready")
        self.hT_done = sem("hT_done")
        self.hT_copied = sem("hT_copied")
        self.z_done = sem("z_done")
        self.z_hi_done = sem("z_hi_done")
        self.z_ready = sem("z_ready")
        self.z_spilled = [sem(f"z_spilled{h}") for h in range(2)]


    def load(self, sp, x1_t, m, slot):
        sp.dma_start(self.x_ln[:, slot, :], x1_t[m]).then_inc(self.ln_loaded[slot], 16)

    def spill(self, sp, first, last, g):
        if first == 0:
            sp.wait_ge(self.z_ready, (g + 1) * self.Q)
        for n in range(first, last):
            half, k, part = n // (2 * self.K), n // 2 % self.K, n % 2
            sp.dma_start(self.spilled[half, part, k].rearrange("f t n -> t f n"),
                         (self.z_hi, self.z_lo)[part][:, half * self.K + k, :]).then_inc(self.z_spilled[half], 16)

    def constants(self, pool):
        pool.memset(self.hmhalf[:], -0.5).then_inc(self.const_ready, 1)
        pool.memset(self.heps[:], EPS).then_inc(self.const_ready, 1)
        pool.wait_ge(self.const_ready, 2)

    def scale(self, pool, m):
        n = held(pool, m + 1)
        pool.wait_ge(self.h_mv, n)
        pool.tensor_tensor(self.hr[:, 0:1], self.hmv[:, 1:2], self.heps[:], ALU.add).then_inc(self.h_eps, 1)
        pool.wait_ge(self.h_eps, n)
        pool.tensor_tensor(self.hr[:, 1:2], self.hr[:, 0:1], self.hmhalf[:], ALU.pow).then_inc(self.h_rstd, 1)

    def high(self, act, m):
        act.wait_ge(self.h_normed, m + 1)
        if not (isinstance(m, int) and m == 0):
            act.wait_ge(self.hT_done, m)
        act.activation(self.h_hi[:], self.xn[:, 0, :], ACT.Copy, scale=XN_SCALE).then_inc(self.h_hi_done, 1)

    def z_high(self, act, m, q, groups_before, banks):
        K = self.K
        if q == 0 and not (isinstance(groups_before, int) and groups_before == 0):
            for half in range(2):
                act.wait_ge(self.z_spilled[half], groups_before * self.SPILLS // 2 * 16)
        for half in range(2):
            act.wait_ge(self.z_done, m * 2 + half + 1)
            act.activation(self.z_hi[:, half * K:(half + 1) * K, q * P:(q + 1) * P],
                           banks[half].rearrange("p (k n) -> p k n", n=P), ACT.Copy,
                           scale=Z_SCALE / (XN_SCALE * FEATURE_SCALE)).then_inc(self.z_hi_done, 1)

    def stats(self, dve, m, slot, count):
        n = held(dve, m + 1)
        dve.wait_ge(self.ln_loaded[slot], count * 16)
        dve.bn_stats(self.hstats[:], self.x_ln[:, slot, :]).then_inc(self.h_bn, 1)
        dve.wait_ge(self.h_bn, n)
        dve.memset(self.hcarrier[:], 0.0)
        dve.bn_aggr(self.hmv[:], self.hstats[:]).then_inc(self.h_mv, 1)

    def norm(self, dve, m, slot):
        dve.wait_ge(self.h_rstd, m + 1)
        dve.tensor_scalar(self.xn[:, 0, :], self.x_ln[:, slot, :], self.hmv[:, 0:1], self.hr[:, 1:2],
                          ALU.subtract, ALU.mult).then_inc(self.h_normed, 1)

    def low(self, dve, m):
        dve.wait_ge(self.h_hi_done, m + 1)
        dve.scalar_tensor_tensor(out=self.h_lo[:], in0=self.xn[:, 0, :], scalar=XN_SCALE, in1=self.h_hi[:],
                                 op0=ALU.mult, op1=ALU.subtract).then_inc(self.h_ready, 1)

    def turn_copy(self, dve, m, banks):
        dve.wait_ge(self.hT_done, m + 1)
        dve.tensor_copy(self.hT[:].rearrange("p a k n -> p (a k n)"), banks[1].bitcast(F16)).then_inc(self.hT_copied, 1)

    def z_low(self, dve, m, q, banks):
        K = self.K
        for half in range(2):
            dve.wait_ge(self.z_hi_done, m * 2 + half + 1)
            low = dve.scalar_tensor_tensor(out=self.z_lo[:, half * K:(half + 1) * K, q * P:(q + 1) * P],
                                           in0=banks[half].rearrange("p (k n) -> p k n", n=P),
                                           scalar=Z_SCALE / (XN_SCALE * FEATURE_SCALE),
                                           in1=self.z_hi[:, half * K:(half + 1) * K, q * P:(q + 1) * P],
                                           op0=ALU.mult, op1=ALU.subtract)
        low.then_inc(self.z_ready, 1)

    def turn(self, pe, m, banks, ident):
        pe.wait_ge(self.h_ready, m + 1)
        if not (isinstance(m, int) and m == 0):
            pe.wait_ge(self.z_ready, m)
        view = banks[1].bitcast(F16)
        for part, src in ((0, self.h_hi), (1, self.h_lo)):
            for k in range(self.K):
                mm = pe.transpose(view[:, (part * self.K + k) * P:(part * self.K + k + 1) * P],
                                  src[:, k * P:(k + 1) * P], ident[:])
        mm.then_inc(self.hT_done, 1)

    def products(self, pe, m, banks):
        feat, hT = self.feat, self.hT
        pe.wait_ge(self.hT_copied, m + 1)
        for half in range(2):
            cols = slice(half * self.ZCOLS, (half + 1) * self.ZCOLS)
            for k in range(self.K):
                out = banks[half][:, k * P:(k + 1) * P]
                pe.matmul(out, feat[:, 0, k, cols], hT[:, 0, k, :], start=True, stop=False)
                pe.matmul(out, feat[:, 0, k, cols], hT[:, 1, k, :], start=False, stop=False)
                mm = pe.matmul(out, feat[:, 1, k, cols], hT[:, 0, k, :], start=False, stop=True)
            mm.then_inc(self.z_done, 1)


class FfnInputs:

    def __init__(self, ctx, nc, K, tiles):
        def sb(name, shape, dt):
            return ctx.enter_context(nc.sbuf_tensor(name, shape, dt))

        def sem(name):
            return ctx.enter_context(nc.semaphore(name))

        self.half = tiles // 2
        self.s_twice = sb("s_twice", [P, 2, self.half, 2, P], F16)
        self.s_low = sb("s_low", [P, 2, self.half, 2, P], F16)
        self.z0 = sb("z0", [P, tiles, 4 * P], F16)
        self.wd = sb("wd", [P, tiles, 2 * K * P], F16)
        self.order = sb("order", [P, tiles], mybir.dt.int32)
        self.s_loaded = sem("s_loaded")
        self.order_loaded = sem("order_loaded")
        self.z_loaded = [[sem(f"z_loaded{p}{h}") for h in range(2)] for p in range(2)]
        self.wd_loaded = [sem(f"wd_loaded{i}") for i in range(7)]

    def weights_under(self, K, E):
        z, wd = self.z0, self.wd
        T = z.shape[1]
        flat = [u[:].rearrange("p s c w n -> p (s c w n)") for u in (self.s_twice, self.s_low)]
        flat += [z[:, n * T // 2:(n + 1) * T // 2].rearrange("p t n -> p (t n)") for n in range(2)]
        flat += [wd[:, n * T // 4:(n + 1) * T // 4].rearrange("p t n -> p (t n)") for n in range(4)]
        parts = list(zip(flat[0::2], flat[1::2]))
        return [[p[n].bitcast(F32R).rearrange("p (k e) -> p k e", k=K) for p in parts] for n in range(2)]

    def load_units(self, sp, s_dram, rows):
        for side in range(2):
            sp.dma_start(self.s_twice[0:rows, side], s_dram[0, side]).then_inc(self.s_loaded, 16)
            sp.dma_start(self.s_twice[rows:2 * rows, side], s_dram[0, side]).then_inc(self.s_loaded, 16)
            sp.dma_start(self.s_low[0:rows, side], s_dram[1, side]).then_inc(self.s_loaded, 16)

    def load_z(self, sp, feats, g, par):
        z = self.z0 if par == 0 else self.z1
        for half in range(2):
            sp.wait_ge(feats.z_spilled[half], (g + 1) * feats.SPILLS // 2 * 16)
            sp.dma_start(z[:, half * self.half:(half + 1) * self.half, :],
                         feats.spilled[half].rearrange("a k f t n -> (a k f) t n")).then_inc(self.z_loaded[par][half], 16)

    def gather(self, pool, d_dram, t):
        pool.indirect_dma_start(self.wd[:, t, :], None, d_dram.rearrange("t p a e -> (t p) (a e)"),
                                bass.IndirectOffsetOnAxis(ap=self.order[:, t:t + 1], axis=0)
                                ).then_inc(self.wd_loaded[t if t < 4 else 3 + t // 4], 16)


def ffn_block(nc, x1, feats, ffn_in, d_dram, c_gate, c_up, c_out, id16, out):
    N, E = x1.shape
    K = E // P
    TOK = 512
    Q = TOK // P
    GROUPS = N // TOK
    I = ffn_in.order.shape[1]
    HALF = I // 2
    KF = K * FEATURES
    STEPS = GROUPS * I
    GATE, UP = range(2)
    RING = 4
    AHEAD = 6
    x1_t = x1.rearrange("(n p) e -> n p e", p=P)
    out_t = out.rearrange("(n p) e -> n p e", p=P)

    with ExitStack() as ctx:
        def sb(name, shape, dt):
            return ctx.enter_context(nc.sbuf_tensor(name, shape, dt))

        def psum(name, shape, dt):
            return ctx.enter_context(nc.psum_tensor(name, shape, dt))

        def sem(name):
            return ctx.enter_context(nc.semaphore(name))

        x_res = sb("x_res2", [P, Q, E], F32)
        s_twice, s_low, wd, z_loaded = ffn_in.s_twice, ffn_in.s_low, ffn_in.wd, ffn_in.z_loaded
        ffn_in.z1 = sb("z1", [P, I, TOK], F16)
        z = [ffn_in.z0, ffn_in.z1]
        gated = sb("gated", [P, 2, TOK], F32)
        inter = sb("inter", [P, 2, TOK], F32)
        inter_hi = sb("inter_hi", [P, 4, TOK], F16)
        inter_lo = sb("inter_lo", [P, 4, TOK], F16)
        y = sb("y", [P, Q, E], F32)
        ostats = sb("ostats", [P, 2, 6], F32)
        omv = sb("omv", [P, Q, 2], F32)
        orr = sb("orr", [P, Q, 3], F32)
        carrier2 = sb("carrier2", [P, 1], F32)

        gbank, ubank, tbank, zbank = [psum(n, [P, BANK], F32) for n in ("gbank", "ubank", "turned", "zbank")]
        dbank = [psum(f"dbank{q}", [P, BANK], F32) for q in range(Q)]
        z_banks = [zbank[:], tbank[:]]

        res2_loaded = [sem(f"res2_loaded{q}") for q in range(Q)]
        out_stored = [sem(f"out_stored{q}") for q in range(Q)]
        gate_done = sem("gate_done")
        up_done = sem("up_done")
        silu_done = sem("silu_done")
        inter_done = sem("inter_done")
        inter_hi_done = sem("inter_hi_done")
        inter_ready = sem("inter_ready")
        down_done = sem("down_done")
        y_act = sem("y_act")
        y_dve = sem("y_dve")
        o_bn = sem("o_bn")
        o_mv = sem("o_mv")
        o_eps = sem("o_eps")
        o_rstd = sem("o_rstd")
        o_mr = sem("o_mr")
        o_normed = sem("o_normed")
        out_ready = sem("out_ready")


        block = ctx.enter_context(nc.Block())

        def is_last(g):
            return isinstance(g, int) and g == GROUPS - 1

        def schedule(engine, quad):
            quad(0, 0, 0, 0, True, True, False, True)
            with engine.Fori(0, GROUPS // 2 - 1) as pair:
                for par in range(2):
                    g = 2 * pair + par
                    for j in range(1, Q):
                        quad(g, par, pair, j, True, True, False, True)
                    quad(g + 1, 1 - par, pair + par, 0, True, True, True, True)
            g, pair = GROUPS - 2, GROUPS // 2 - 1
            for j in range(1, Q):
                quad(g, 0, pair, j, j < 3, j < 2, False, False)
            quad(g + 1, 1, pair, 0, False, False, True, False)
            for j in range(1, Q):
                quad(g + 1, 1, pair, j, False, False, False, False)

        @block.sync
        def _(sp):
            def load_res(g, q):
                sp.dma_start(x_res[:, q, :], x1_t[g * Q + q]).then_inc(res2_loaded[q], 16)

            def regroup(g, par, loads_before):
                for half in range(2):
                    sp.wait_ge(z_loaded[1 - par][half], loads_before * 16)
                feats.spill(sp, 0, feats.SPILLS, g)
                ffn_in.load_z(sp, feats, g, par)

            def quad(g, par, pair, j, evac_z, prep, finish, stream):
                if stream:
                    m = g * Q + j + AHEAD + 1
                    sp.wait_ge(feats.h_normed, m - RING + 1)
                    feats.load(sp, x1_t, m, (j + AHEAD + 1) % RING)
                if finish:
                    for q in range(Q):
                        sp.wait_ge(out_ready, (g - 1) * Q + q + 1)
                        sp.dma_start(out_t[(g - 1) * Q + q], x_res[:, q, :]).then_inc(out_stored[q], 16)
                    for q in range(Q):
                        sp.wait_ge(out_stored[q], g * 16)
                        load_res(g, q)
                if evac_z and j == 2:
                    regroup(g + 1, 1 - par, pair + 1)

            for q in range(Q):
                load_res(0, q)
            schedule(sp, quad)
            for q in range(Q):
                sp.wait_ge(out_ready, (GROUPS - 1) * Q + q + 1)
                sp.dma_start(out_t[(GROUPS - 1) * Q + q], x_res[:, q, :]).then_inc(out_stored[q], 16)
            for q in range(Q):
                sp.wait_ge(out_stored[q], GROUPS * 16)

        @block.gpsimd
        def _(pool):
            def o_scale(g, q):
                n = held(pool, g * Q + q + 1)
                pool.wait_ge(o_mv, n)
                pool.tensor_tensor(orr[:, q, 0:1], omv[:, q, 1:2], feats.heps[:], ALU.add).then_inc(o_eps, 1)
                pool.wait_ge(o_eps, n)
                pool.tensor_tensor(orr[:, q, 1:2], orr[:, q, 0:1], feats.hmhalf[:], ALU.pow).then_inc(o_rstd, 1)
                pool.wait_ge(o_rstd, n)
                pool.tensor_tensor(orr[:, q, 2:3], omv[:, q, 0:1], orr[:, q, 1:2], ALU.mult).then_inc(o_mr, 1)

            def quad(g, par, pair, j, evac_z, prep, finish, stream):
                if finish:
                    o_scale(g - 1, 0)
                if prep:
                    feats.scale(pool, g * Q + j + AHEAD)
                if finish:
                    for q in range(1, Q):
                        o_scale(g - 1, q)

            pool.wait_ge(ffn_in.order_loaded, 16)
            for t in range(I):
                if t == 1:
                    feats.scale(pool, Q + 1)
                ffn_in.gather(pool, d_dram, t)
            schedule(pool, quad)
            for q in range(Q):
                o_scale(GROUPS - 1, q)

        @block.scalar
        def _(act):
            def high(n, slot):
                act.wait_ge(inter_done, n + 1)
                if not (isinstance(n, int) and n < 4):
                    act.wait_ge(down_done, n * Q - 3 * Q)
                act.copy(inter_hi[:, slot, :], inter[:, slot % 2, :]).then_inc(inter_hi_done, 1)

            def silu_at(n, slot):
                act.wait_ge(gate_done, n + 1)
                act.activation(gated[:, slot % 2, :], gbank[:], ACT.Silu, scale=c_gate[:]).then_inc(silu_done, 1)

            def o_norm(g, q):
                act.wait_ge(o_rstd, g * Q + q + 1)
                act.activation(y[:, q, :], y[:, q, :], ACT.Copy, scale=orr[:, q, 1:2]).then_inc(o_normed, 1)

            def quad(g, par, pair, j, evac_z, prep, finish, stream):
                for s in range(4):
                    i = 4 * j + s
                    n = g * I + i
                    last = isinstance(n, int) and n >= STEPS - 2
                    if not (last and n == STEPS - 1):
                        if isinstance(n, int) and n == 0:
                            high(1, 1)
                        else:
                            high(n + 1, (s + 1) % 4)
                    if not last:
                        silu_at(n + 2, (s + 2) % 4)
                    if finish and s:
                        o_norm(g - 1, s - 1)
                    if finish and s == 3:
                        o_norm(g - 1, 3)
                    if s == 0 and evac_z:
                        feats.z_high(act, g * Q + j + AHEAD - 1, (j + 1) % Q, g + 2, z_banks)
                    if s == 1 and prep:
                        feats.high(act, g * Q + j + AHEAD)
                    if i == I - 1:
                        for q in range(Q) if is_last(g) else (0, 2):
                            act.wait_ge(down_done, n * Q + q + 1)
                            act.activation(y[:, q, :], dbank[q][:], ACT.Copy, scale=c_out[:]).then_inc(y_act, 1)

            silu_at(0, 0)
            feats.high(act, Q + 1)
            high(0, 0)
            silu_at(1, 1)
            schedule(act, quad)
            for q in range(Q):
                o_norm(GROUPS - 1, q)

        @block.vector
        def _(dve):
            def product(n, slot):
                dve.wait_ge(silu_done, n + 1)
                dve.wait_ge(up_done, n + 1)
                dve.scalar_tensor_tensor(out=inter[:, slot % 2, :], in0=ubank[:], scalar=c_up[:],
                                         in1=gated[:, slot % 2, :], op0=ALU.mult, op1=ALU.mult).then_inc(inter_done, 1)

            def low(n, slot):
                dve.wait_ge(inter_hi_done, n + 1)
                dve.tensor_tensor(inter_lo[:, slot, :], inter[:, slot % 2, :], inter_hi[:, slot, :],
                                  ALU.subtract).then_inc(inter_ready, 1)

            def o_stats(g, q):
                n = held(dve, g * Q + q + 1)
                if is_last(g):
                    dve.wait_ge(y_act, g * 2 + q + 1)
                elif q % 2 == 0:
                    dve.wait_ge(y_act, g * 2 + q // 2 + 1)
                else:
                    dve.wait_ge(y_dve, g * 2 + q // 2 + 1)
                dve.bn_stats(ostats[:, q % 2, :], y[:, q, :]).then_inc(o_bn, 1)
                dve.wait_ge(o_bn, n)
                dve.memset(carrier2[:], 0.0)
                dve.bn_aggr(omv[:, q, :], ostats[:, q % 2, :]).then_inc(o_mv, 1)

            def o_finish(g, q):
                n = g * Q + q + 1
                dve.wait_ge(res2_loaded[q], (g + 1) * 16)
                dve.wait_ge(o_mr, n)
                dve.wait_ge(o_normed, n)
                dve.scalar_tensor_tensor(out=x_res[:, q, :], in0=y[:, q, :], scalar=orr[:, q, 2:3],
                                         in1=x_res[:, q, :], op0=ALU.subtract, op1=ALU.add).then_inc(out_ready, 1)

            def quad(g, par, pair, j, evac_z, prep, finish, stream):
                m, slot = g * Q + j + AHEAD, (j + AHEAD) % RING
                count = g + 1 + (j + AHEAD) // RING
                for s in range(4):
                    i = 4 * j + s
                    n = g * I + i
                    if s == 3 and prep:
                        feats.turn_copy(dve, m, z_banks)
                    if not (isinstance(n, int) and n == STEPS - 1):
                        low(n + 1, (s + 1) % 4)
                    if not (isinstance(n, int) and n >= STEPS - 2):
                        product(n + 2, (s + 2) % 4)
                    if s == 0 and evac_z:
                        feats.z_low(dve, m - 1, (j + 1) % Q, z_banks)
                    if finish:
                        o_stats(g - 1, s)
                        if s:
                            o_finish(g - 1, s - 1)
                        if s == 3:
                            o_finish(g - 1, 3)
                    if s == 0 and prep:
                        feats.stats(dve, m, slot, count)
                    if s == 1 and prep:
                        feats.norm(dve, m, slot)
                        feats.low(dve, m)
                    if i == I - 1 and not is_last(g):
                        for q in (1, 3):
                            dve.wait_ge(down_done, n * Q + q + 1)
                            dve.tensor_scalar(y[:, q, :], dbank[q][:], c_out[:], None, ALU.mult).then_inc(y_dve, 1)

            feats.stats(dve, Q + 1, 1, 2)
            feats.norm(dve, Q + 1, 1)
            feats.low(dve, Q + 1)
            product(0, 0)
            low(0, 0)
            product(1, 1)
            feats.turn_copy(dve, Q + 1, z_banks)
            schedule(dve, quad)
            for q in range(Q):
                o_stats(GROUPS - 1, q)
                if q:
                    o_finish(GROUPS - 1, q - 1)
            o_finish(GROUPS - 1, Q - 1)

        @block.tensor
        def _(pe):

            def gate_up(n, i, par, count):
                if i % HALF == 0:
                    pe.wait_ge(z_loaded[par][i // HALF], count * 16)
                side, c = i // HALF, i % HALF
                for w, bank, free, done in ((GATE, gbank, silu_done, gate_done), (UP, ubank, inter_done, up_done)):
                    if not (isinstance(n, int) and n == 0):
                        pe.wait_ge(free, n)
                    pe.matmul(bank[:], s_twice[:, side, c, w, :], z[par][:, i, :], start=True, stop=False)
                    pe.matmul(bank[:], s_low[0:KF, side, c, w, :], z[par][0:KF, i, :], start=False, stop=True
                              ).then_inc(done, 1)

            def down(g, n, i):
                if isinstance(n, int) and n < 4:
                    pe.wait_ge(ffn_in.wd_loaded[n], 16)
                pe.wait_ge(inter_ready, n + 1)
                s = i % 4
                for q in range(Q):
                    if i == 0 and not (isinstance(g, int) and g == 0):
                        pe.wait_ge((y_act, y_dve)[q % 2], g * 2 - 1 + q // 2)
                    c = slice(q * P, (q + 1) * P)
                    start, stop = i == 0, i == I - 1
                    pe.matmul(dbank[q][:], inter_hi[:, s, c], wd[:, i, 0:E], start=start, stop=False)
                    pe.matmul(dbank[q][:], inter_hi[:, s, c], wd[:, i, E:2 * E], start=False, stop=False)
                    pe.matmul(dbank[q][:], inter_lo[:, s, c], wd[:, i, 0:E], start=False, stop=stop
                              ).then_inc(down_done, 1)

            def quad(g, par, pair, j, evac_z, prep, finish, stream):
                m = g * Q + j + AHEAD
                if j:
                    pe.wait_ge(ffn_in.wd_loaded[3 + j], 4 * 16)
                for s in range(4):
                    i = 4 * j + s
                    n = g * I + i
                    if i + 2 < I:
                        gate_up(n + 2, i + 2, par, pair + 1)
                    elif not (isinstance(n, int) and n >= STEPS - 2):
                        gate_up(n + 2, i + 2 - I, 1 - par, pair + 1 + par)
                    down(g, n, i)
                    if s == 2 and prep:
                        feats.turn(pe, m, z_banks, id16)
                    if s == 3 and prep:
                        feats.products(pe, m, z_banks)

            pe.wait_ge(ffn_in.s_loaded, 6 * 16)
            gate_up(0, 0, 0, 1)
            gate_up(1, 1, 0, 1)
            feats.turn(pe, Q + 1, z_banks, id16)
            feats.products(pe, Q + 1, z_banks)
            schedule(pe, quad)


def piece_grid(n_ctrl, n_samples, r):
    import numpy as np
    step = (n_ctrl - 1.0) / (n_samples - 1)
    seg = np.minimum(np.floor(step * P * r).astype(np.int64), n_ctrl - 2)
    n = P * r[None, :] + np.arange(P)[:, None]
    later = np.minimum(np.floor(step * n).astype(np.int64), n_ctrl - 2) - seg
    assert ((later == 0) | (later == 1)).all()
    return step, seg, later


def piece_powers(step, r, seg, later):
    import numpy as np
    catmull = 0.5 * np.array([[0, 2, 0, 0], [-1, 0, 1, 0], [2, -5, 4, -1], [-1, 3, -3, 1]], np.float64)
    binom = np.array([[1, 0, 0, 0], [1, 1, 0, 0], [1, 2, 1, 0], [1, 3, 3, 1]], np.float64)
    half = P // 2
    mid = step * (P * r + half) - seg - later
    return np.stack([np.stack([sum(catmull[j, q] * binom[j, m] * mid ** (j - m) for j in range(m, 4))
                               * (step * half) ** m for q in range(4)]) for m in range(4)])


def fold(a, parts):
    import numpy as np
    return np.concatenate(np.split(a, parts, axis=-1), axis=0)


def row_tables(r, n_ctrl, n_samples):
    import numpy as np
    step, seg, later = piece_grid(n_ctrl, n_samples, r)
    points = np.empty((32, r.size), np.int64)
    coef = np.empty((32, r.size), np.float64)
    for nxt in range(2):
        powers = piece_powers(step, r, seg, nxt)
        for m in range(4):
            for q in range(4):
                row = 16 * nxt + 4 * m + q
                points[row] = np.clip(seg + nxt + q - 1, 0, n_ctrl - 1)
                coef[row] = powers[m, q]
    return fold(points, 4), fold(coef, 4).astype(np.float32), fold(later.astype(np.uint8), 1)


def vandermonde():
    import numpy as np
    v = (np.arange(P) - P // 2) / (P // 2)
    table = np.zeros((P, 2, P), np.float32)
    for g in range(4):
        for nxt in range(2):
            for m in range(4):
                for q in range(4):
                    table[32 * g + 16 * nxt + 4 * m + q, nxt] = v ** m
    return table


def phase_order(n_ctrl, n_samples, K):
    import numpy as np
    step = (n_ctrl - 1.0) / (n_samples - 1)
    units = n_samples // (K * P)
    return np.argsort(-np.mod(step * K * P * np.arange(units), 1), kind="stable")


def feature_tables(order, K, n_ctrl, n_samples):
    import numpy as np
    T = order.size // P
    v = (np.arange(P) - P // 2) / (P // 2)
    feat = np.zeros((P, K, T, FEATURES), np.float64)
    coef = np.zeros((K, FEATURES, 5, order.size), np.float64)
    points = np.zeros((K, FEATURES, 5, order.size), np.int64)
    for k in range(K):
        r = K * order + k
        step, seg, later = piece_grid(n_ctrl, n_samples, r)
        for q in range(5):
            points[k, :, q] = np.clip(seg - 1 + q, 0, n_ctrl - 1)
        powers = [piece_powers(step, r, seg, nxt) for nxt in range(2)]
        for t in range(T):
            cols = slice(t * P, (t + 1) * P)
            kinds, kind, count = np.unique(later[:, cols], axis=0, return_inverse=True, return_counts=True)
            kind = kind.ravel()
            ranges = np.argsort(-count, kind="stable")[:2]
            for a, which in enumerate(ranges):
                inside = kind == which
                for m in range(4):
                    feat[inside, k, t, 4 * a + m] = v[inside] ** m
                    for c in range(P):
                        nxt = kinds[which, c]
                        coef[k, 4 * a + m, nxt:nxt + 4, t * P + c] = powers[nxt][m, :, t * P + c]
            window = np.flatnonzero(~np.isin(kind, ranges))
            assert window.size <= FEATURES - 8
            for w, p in enumerate(window):
                feat[p, k, t, 8 + w] = 1.0
                for c in range(P):
                    nxt = later[p, t * P + c]
                    coef[k, 8 + w, nxt:nxt + 4, t * P + c] = (v[p] ** np.arange(4)) @ powers[nxt][:, :, t * P + c]
    assert np.abs(coef).sum(2).max() < 7.9
    feat *= FEATURE_SCALE
    high = feat.astype(np.float16)
    low = (feat - high).astype(np.float16)
    assert (high.astype(np.float64) + low == feat).all()
    features = np.stack([high, low], 1).reshape(P, 2, K, T * FEATURES)
    return features, points.reshape(K * FEATURES, 5, -1), coef.reshape(K * FEATURES, 5, -1).astype(np.float32)


def build(nc, x, wq, wk, wvT, wo, raw_ctrl, unit_ctrl, unit_coef, row_ctrl, row_coef, later_half, vander,
          features, perm, out):
    tiles, kf = perm.shape[1], unit_coef.shape[1] // 2
    hidden = x.shape[2]
    x1 = nc.dram_tensor("x1", out.shape, F32, kind="Internal").ap()
    s_dram = nc.dram_tensor("unit_features", (2, 2, kf, unit_coef.shape[0], 2, unit_coef.shape[3]), F16,
                            kind="Internal").ap()
    d_dram = nc.dram_tensor("down_rows", (tiles, P, 2, hidden), F16, kind="Internal").ap()
    z_spill = nc.dram_tensor("token_features", (2, 2, hidden // P, FEATURES, tiles // 2, 512), F16,
                             kind="Internal").ap()
    with ExitStack() as ctx:
        c_gate, c_up, c_out = [ctx.enter_context(nc.sbuf_tensor(name, [P, 1], F32))
                               for name in ("c_gate", "c_up", "c_out")]
        feats = TokenFeatures(ctx, nc, hidden // P, tiles, z_spill)
        ffn_in = FfnInputs(ctx, nc, hidden // P, tiles)
        id16 = ctx.enter_context(nc.sbuf_tensor("ident16", [P, P], F16))
        attention_block(nc, x, wq, wk, wvT, wo, x1, raw_ctrl, unit_ctrl, unit_coef, row_ctrl, row_coef, later_half,
                        vander, s_dram, d_dram, c_gate, c_up, c_out, features, feats, ffn_in, perm, id16)
        ffn_block(nc, x1, feats, ffn_in, d_dram, c_gate, c_up, c_out, id16, out)


def kernel(**inputs):
    import numpy as np
    import concourse.bacc as bacc
    from concourse.bass_utils import run_bass_kernel_spmd as run

    nc = bacc.Bacc("TRN2", target_bir_lowering=False, num_devices=1)
    arrays = {}

    def dram(name, a):
        arrays[name] = np.ascontiguousarray(a)
        return nc.dram_tensor(name, arrays[name].shape, mybir.dt.from_np(arrays[name].dtype), kind="ExternalInput").ap()

    x = np.asarray(inputs["L0_attn_x"])
    hidden = x.shape[-1]
    cps = [np.asarray(inputs[f"L0_ffn_{n}_cp"]) for n in ("gate", "up", "down")]
    n_ctrl = cps[0].shape[0]
    ffn = 4 * hidden
    K, I = hidden // P, ffn // P
    order = phase_order(n_ctrl, ffn * hidden, K)
    features, unit_points, unit_coef = feature_tables(order, K, n_ctrl, ffn * hidden)
    i, h = np.meshgrid(np.arange(I), np.arange(hidden), indexing="ij")
    row_points, row_coef, later = row_tables((I * h + i).ravel(), n_ctrl, ffn * hidden)
    every = np.minimum(np.arange(-(-n_ctrl // P) * P), n_ctrl - 1).reshape(P, -1)
    B = x.shape[0]

    def chunks(a, n):
        return np.stack(np.split(a, n, axis=-1))

    args = [
        dram("x", x), dram("wq", inputs["L0_attn_Wq"]), dram("wk", inputs["L0_attn_Wk"]),
        dram("wvT", np.asarray(inputs["L0_attn_Wv"]).T), dram("wo", inputs["L0_attn_Wo"]),
        dram("raw_ctrl", np.stack([c[every] for c in cps], 1)),
        dram("unit_ctrl", chunks(np.stack([fold(c[unit_points], 2) for c in cps[:2]], 1), 2 * B).reshape(2 * B, P, -1)),
        dram("unit_coef", chunks(fold(unit_coef, 2), 2 * B)),
        dram("row_ctrl", chunks(cps[2][row_points], B)), dram("row_coef", chunks(row_coef, B)),
        dram("later_half", later.reshape(P, 4, B, hidden).transpose(2, 0, 1, 3).reshape(B, P, -1).view(np.int32)),
        dram("vander", vandermonde()), dram("features", features),
        dram("perm", order.reshape(I, P).T.astype(np.int32)),
    ]
    out = nc.dram_tensor("out", (x.shape[0] * x.shape[1], hidden), F32, kind="ExternalOutput").ap()
    build(nc, *args, out)
    result = run(nc, [arrays], core_ids=[0])
    return result.results[0]["out"].reshape(x.shape)
```
